# Optimizing a Trainium2 kernel written in Bass

```python
import numpy as np
import jax
import jax.numpy as jnp

def _softmax(x, axis=-1):
    return jax.nn.softmax(x, axis=axis)
def _gelu(x):
    return jax.nn.gelu(x, approximate=True)
def _silu(x):
    return jax.nn.silu(x)
def _sigmoid(x):
    return jax.nn.sigmoid(x)
def _layernorm(x, axis=-1, eps=1e-5):
    m = jnp.mean(x, axis=axis, keepdims=True)
    v = jnp.var(x, axis=axis, keepdims=True)
    return (x - m) / jnp.sqrt(v + eps)
def _scatter_add(tgt, idx, src, axis=0):
    return tgt.at[idx].add(src)
def _segment_sum(src, seg, n):
    return jax.ops.segment_sum(src, seg, n)

kernel_name = 'mk_adj_preln_d2_adj_64_eb52b3'

def setup_inputs(seed: int = 0):
    np.random.seed(seed)
    _w = jnp.asarray
    def _rec_inputs():
        import jax
        import jax.numpy as jnp
        _gk = jax.random.key(seed)
        x = -0.006082 + 1.001 * jax.random.normal(jax.random.fold_in(_gk, 1), (128, 128, 64), jnp.float32)
        _a = jax.random.bernoulli(jax.random.fold_in(_gk, 2), 0.0625, (128, 128, 128))
        _a = jnp.logical_or(_a, jnp.swapaxes(_a, -1, -2))
        _a = jnp.logical_or(_a, jnp.eye(128, dtype=bool))
        _af = _a.astype(jnp.float32)
        _af = _af * jax.random.uniform(jax.random.fold_in(_gk, 3), (128, 128, 128), jnp.float32, 0.05, 4.42607)
        adj = _af
        return x, adj
    x, adj = _rec_inputs()
    def _L0_gnn_setup():
        import jax, jax.numpy as jnp
        import numpy as np
        key = jax.random.key(seed)
        ks = jax.random.split(key, 6)
        B, N, F, H, O = (2, 512, 64, 192, 64)
        x = jax.random.normal(ks[0], (B, N, F), dtype=jnp.float32)
        adj = jax.random.normal(ks[1], (B, N, N), dtype=jnp.float32)
        W1 = jax.random.normal(ks[2], (2 * F, H), dtype=jnp.float32) * (1.0 / np.sqrt(2 * F))
        b1 = jax.random.normal(ks[3], (H,), dtype=jnp.float32) * 0.02
        W2 = jax.random.normal(ks[4], (H, O), dtype=jnp.float32) * (1.0 / np.sqrt(H))
        b2 = jax.random.normal(ks[5], (O,), dtype=jnp.float32) * 0.02
        return {'x': x, 'adj': adj, 'W1': W1, 'b1': b1, 'W2': W2, 'b2': b2}
    _L0_gnn_all = _L0_gnn_setup()
    _L0_gnn_in = {k: v for k, v in _L0_gnn_all.items() if k in ('W1', 'b1', 'W2', 'b2', )}
    del _L0_gnn_all

    def _L1_gnn_setup():
        import jax, jax.numpy as jnp
        import numpy as np
        B, N, F_IN, F_OUT = (32, 2048, 64, 64)
        key = jax.random.key(seed)
        k1, k2, k3 = jax.random.split(key, 3)
        vertices = jax.random.normal(k1, (B, N, F_IN), dtype=jnp.float32)
        g_mat = jax.random.uniform(k2, (B, N, N), dtype=jnp.float32)
        W = jax.random.normal(k3, (F_OUT, F_IN), dtype=jnp.float32) * (1.0 / np.sqrt(F_IN))
        return {'vertices': vertices, 'g_mat': g_mat, 'W': W}
    _L1_gnn_all = _L1_gnn_setup()
    _L1_gnn_in = {k: v for k, v in _L1_gnn_all.items() if k in ('W', )}
    del _L1_gnn_all

    return {
        "x": x,
        "adj": adj,
        "L0_gnn_W1": _L0_gnn_in["W1"],
        "L0_gnn_b1": _L0_gnn_in["b1"],
        "L0_gnn_W2": _L0_gnn_in["W2"],
        "L0_gnn_b2": _L0_gnn_in["b2"],
        "L1_gnn_W": _L1_gnn_in["W"],
    }

def reference(x, adj, L0_gnn_W1, L0_gnn_b1, L0_gnn_W2, L0_gnn_b2, L1_gnn_W):
    import jax
    import jax.numpy as jnp
    def _L0_gnn_ref(x, adj, W1, b1, W2, b2):
        import jax, jax.numpy as jnp
        import numpy as np
        F = x.shape[-1]
        mask = (adj > 0.0).astype(x.dtype)
        W1a, W1b = (W1[:F], W1[F:])
        xj_proj = x @ W1a
        diff = x[:, :, None, :] - x[:, None, :, :]
        h = jax.nn.relu(xj_proj[:, :, None, :] + diff @ W1b + b1)
        hm = jnp.einsum('bjkh,bjk->bjh', h, mask)
        deg = jnp.sum(mask, axis=-1)
        return hm @ W2 + deg[..., None] * b2

    def _L1_gnn_ref(vertices, g_mat, W):
        import jax, jax.numpy as jnp
        import numpy as np
        B, N, F_IN, F_OUT = (32, 2048, 64, 64)
        agg = jnp.einsum('bnm,bmf->bnf', g_mat, vertices)
        out = jnp.einsum('bnf,of->bno', agg, W)
        return out

    h = jnp.maximum(_layernorm(x, axis=-1), 0.0)
    x = x + _L0_gnn_ref(h, adj, L0_gnn_W1, L0_gnn_b1, L0_gnn_W2, L0_gnn_b2)
    h = jnp.maximum(_layernorm(x, axis=-1), 0.0)
    x = x + _L1_gnn_ref(h, adj, L1_gnn_W)
    return x


_drawn_inputs = setup_inputs


def setup_inputs(seed=0):
    import zlib

    import numpy as np

    out = dict(_drawn_inputs(seed))
    spreads = {}
    factors = {}
    for name, (base, spread) in spreads.items():
        noise = np.random.default_rng([zlib.crc32(name.encode()), seed]).standard_normal(out[name].shape)
        drawn = base * np.exp(spread * noise) if base else spread * noise
        out[name] = jnp.asarray(drawn.astype(out[name].dtype))
    for name, factor in factors.items():
        out[name] = (out[name] * factor).astype(out[name].dtype)
    return out
```

```python
from contextlib import ExitStack

import concourse.bass as bass
from concourse import mybir

F32 = mybir.dt.float32
BF16 = mybir.dt.bfloat16
I32 = mybir.dt.int32
ALU = mybir.AluOpType
ACT = mybir.ActivationFunctionType
AX_X = mybir.AxisListType.X

EPS = 1e-5
SLOTS = 4
BANKS = 2
PER_BANK = SLOTS // BANKS
RING = 3
ALWAYS = 6
STATIC = 8
PARTS = 8
BODY = 4


def gnn_kernel(nc, x, adjT, W1a, W1b, b1, W2, b2, W3T, ident, before, slot_no, out):
    N, B, F = x.shape
    H = W1a.shape[1]
    O = W2.shape[1]
    H2 = H - N
    ROW = PER_BANK * H
    STRIDE = BANKS * 512
    PER_PART = B // PARTS
    assert N == 128 and B == N and F == O and N < H <= 256 and ROW <= 512 and 2 * H + N <= 512

    with ExitStack() as ctx:
        def sb(name, shape, dt=F32):
            return ctx.enter_context(nc.sbuf_tensor(name, shape, dt))

        def sem(name):
            return ctx.enter_context(nc.semaphore(name))

        x_all = sb("x_all", [N, B, F])
        adj_all = sb("adj_all", [N, B, N])
        mask_all = sb("mask_all", [N, B, N], BF16)
        rank_all = mask_all
        w_pq = sb("w_pq", [F + 1, 2 * H])
        w1b = sb("w1b", [F, H])
        w2a = sb("w2a", [N, O])
        w2b = sb("w2b", [H2, O])
        w3t = sb("w3t", [F, O])
        b2_rows = sb("b2_rows", [N, O])
        consts = sb("consts", [N, 3, N])
        upto = sb("upto", [N, N], BF16)
        ones = sb("ones", [N, 1], BF16)
        half_power = sb("half_power", [N, N])
        stats1 = sb("stats1", [N, B, 6])
        mom = sb("mom", [N, 4, B])
        rstd1 = sb("rstd1", [N, B])
        shift1 = sb("shift1", [N, B])
        deg = sb("deg", [N, B])
        cnt = sb("cnt", [N, 3 + RING])
        cnt_i = sb("cnt_i", [N, 2], I32)
        cnt_rows = sb("cnt_rows", [N, 2, N])
        counts = sb("counts", [1, 3, B], I32)
        spare = sb("spare", [N, B])
        h1 = sb("h1", [N, F])
        h1T = sb("h1T", [F + 1, N])
        P = sb("P", [N, 2, H])
        Q = sb("Q", [N, 2, 3, H], BF16)
        q_rest = sb("q_rest", [N, H])
        onehot = sb("onehot", [N, 2, STATIC * SLOTS, 2, N], BF16)
        onehot_loop = sb("onehot_loop", [N, SLOTS, N], BF16)
        start = sb("start", [N, 2, BANKS, ROW])
        acc = sb("acc", [N, 2, BANKS, ROW])
        half = sb("half", [N, ROW])
        hm = sb("hm", [N, H])
        hmT = sb("hmT", [N, 2, N])
        stats2 = sb("stats2", [N, 6])
        mv = sb("mv", [N, 2, 2])
        ve2 = sb("ve2", [N, 1])
        neg2 = sb("neg2", [N, 1])
        rstd2 = sb("rstd2", [N, 2])
        shift2 = sb("shift2", [N, 2])
        h2 = sb("h2", [N, F])
        aggT = sb("aggT", [F, N])

        ring = ctx.enter_context(nc.psum_tensor("ring", [N, RING * BANKS, 512], F32))
        prep = ctx.enter_context(nc.psum_tensor("prep", [N, 512], F32))
        post = ctx.enter_context(nc.psum_tensor("post", [N, 512], F32))
        ring_flat = ring[:].rearrange("p a b -> p (a b)")
        pq_ps, h1T_ps = prep[:, 0:2 * H], prep[0:F, 2 * H:2 * H + N]
        hmT_ps, out1_ps = post[:, 0:2 * N], post[:, 2 * N:2 * N + O]
        aggT_ps, out2_ps = post[0:F, 320:320 + N], post[:, 320 + N:320 + N + O]

        consts_in = sem("consts_in")
        x_in = sem("x_in")
        adj_in = [sem(f"adj_in{g}") for g in range(PARTS)]
        weights_ready = sem("weights_ready")
        mask_ready = sem("mask_ready")
        rank_sums = sem("rank_sums")
        rank_ready = sem("rank_ready")
        deg_sums = sem("deg_sums")
        deg_ready = sem("deg_ready")
        degT_ready = sem("degT_ready")
        chunk_counts = sem("chunk_counts")
        count_sums = sem("count_sums")
        counts_ready = sem("counts_ready")
        moments_ready = sem("moments_ready")
        norm1_ready = sem("norm1_ready")
        dve_step = sem("dve_step")
        pool_step = sem("pool_step")
        h1_ready = sem("h1_ready")
        h1T_sums = sem("h1T_sums")
        h1T_ready = sem("h1T_ready")
        pq_sums = sem("pq_sums")
        p_ready = sem("p_ready")
        rest_ready = sem("rest_ready")
        mid_ready = sem("mid_ready")
        q_ready = sem("q_ready")
        start_ready = sem("start_ready")
        onehot_ready = sem("onehot_ready")
        onehot_loop_ready = sem("onehot_loop_ready")
        seeded = sem("seeded")
        gathered = sem("gathered")
        ring_free = sem("ring_free")
        half_ready = sem("half_ready")
        hm_ready = sem("hm_ready")
        hmT_sums = sem("hmT_sums")
        hmT_ready = sem("hmT_ready")
        out1_sums = sem("out1_sums")
        xb_ready = sem("xb_ready")
        x1_ready = sem("x1_ready")
        stats2_ready = sem("stats2_ready")
        mv_ready = sem("mv_ready")
        ve2_ready = sem("ve2_ready")
        rstd2_ready = sem("rstd2_ready")
        neg2_ready = sem("neg2_ready")
        norm2_ready = sem("norm2_ready")
        h2_ready = sem("h2_ready")
        aggT_sums = sem("aggT_sums")
        aggT_ready = sem("aggT_ready")
        out2_sums = sem("out2_sums")
        y_ready = sem("y_ready")
        stored = sem("stored")

        HEAD, TAIL = 2, 3
        N_CONSTS = 10

        def graphs(eng, step):
            for b in range(-HEAD, BODY):
                step(b, b % BODY)
            with eng.Fori(1, B // BODY - 1) as t:
                for u in range(BODY):
                    step(t * BODY + u, u)
            for b in range(B - BODY, B + TAIL):
                step(b, b % BODY)

        def exists(b):
            return not isinstance(b, int) or 0 <= b < B

        def chunks_before(eng, b):
            return eng.value_load(counts[0:1, 0, bass.ds(b, 1)], min_val=0, max_val=B * N // SLOTS)

        def chunks_of(eng, b):
            return eng.value_load(counts[0:1, 1, bass.ds(b, 1)], min_val=ALWAYS, max_val=N // SLOTS)

        def loops_before(eng, b):
            return eng.value_load(counts[0:1, 2, bass.ds(b, 1)], min_val=0, max_val=B * N // SLOTS)

        def wait_apart(eng, semaphore, value):
            if not isinstance(value, int):
                eng.reg_mov(until[eng.engine], value)
                eng.wait_ge(weights_ready, 1)
                value = until[eng.engine]
            eng.wait_ge(semaphore, value)

        def places(eng, base):
            return [eng.snap(((base + r) % RING) * STRIDE) for r in range(RING)]

        until = {}
        for eng in (nc.tensor, nc.scalar, nc.vector, nc.gpsimd):
            until[eng.engine] = eng.alloc_register("until")

        block = ctx.enter_context(nc.Block())

        @block.sync
        def _(sp):
            with nc.allow_non_contiguous_dma("small weights"):
                for dst, src in ((consts[:, 0, :], before), (consts[:, 1, :], ident), (consts[:, 2, :], slot_no),
                                 (w_pq[0:F, 0:H], W1a), (w_pq[F:F + 1, 0:H], b1), (w1b[:, :], W1b),
                                 (w2a[:, :], W2[0:N, :]), (w2b[:, :], W2[N:H, :]), (w3t[:, :], W3T),
                                 (b2_rows[:, :], b2.partition_broadcast(N))):
                    sp.dma_start(dst, src).then_inc(consts_in, 16)
            sp.dma_start(x_all[:, :, :], x).then_inc(x_in, 16)
            for g in range(PARTS):
                b = slice(g * PER_PART, (g + 1) * PER_PART)
                sp.dma_start(adj_all[:, b, :], adjT[:, b, :]).then_inc(adj_in[g], 16)
            with sp.Fori(0, B // BODY) as t:
                sp.wait_ge(y_ready, t * BODY + BODY)
                b = bass.ds(t * BODY, BODY)
                sp.dma_start(out[:, b, :], x_all[:, b, :]).then_inc(stored, 16)
            sp.wait_ge(stored, 16 * B // BODY)

        @block.tensor
        def _(pe):
            pe.wait_ge(weights_ready, 1)
            with pe.Fori(0, PARTS) as g:
                pe.wait_ge(mask_ready, g + 1)
                for q in range(PER_PART // 4):
                    pe.wait_ge(rank_ready, g * (PER_PART // 4) + q + 1)
                    quad = mask_all[:, bass.ds(g * PER_PART + 4 * q, 4), :]
                    nc.tensor.matmul(ring[:, q, :], upto[:, :], quad, start=True, stop=True).then_inc(rank_sums, 1)
                for i in range(PER_PART):
                    b = g * PER_PART + i
                    last = nc.tensor.matmul(prep[:, bass.ds(b, 1)], mask_all[:, b, :], ones[:, :], start=True, stop=True)
                last.then_inc(deg_sums, 1)
            for q in range(PER_PART // 4, RING * BANKS):
                last = nc.tensor.matmul(ring[:, q, :], upto[:, :], mask_all[:, 0:4, :], start=True, stop=True)
            pe.wait_ge(deg_ready, 1)
            nc.tensor.transpose(post[:, 0:N], deg[:, :], consts[:, 1, :]).then_inc(degT_ready, 1)
            pe.wait_ge(chunk_counts, 1)
            nc.tensor.matmul(post[:, 0:2 * N], cnt_rows[:, 0, :], consts[:, 0:2, :], start=True, stop=True)
            nc.tensor.matmul(post[:, 2 * N:3 * N], cnt_rows[:, 1, :], consts[:, 0, :], start=True,
                             stop=True).then_inc(count_sums, 1)

            def gather(c, to, parts, hot):
                pe.wait_ge(seeded, c + 1)
                for s in range(SLOTS):
                    at = to + (s // PER_BANK) * 512 + (s % PER_BANK) * H
                    for part in range(3):
                        last = nc.tensor.matmul(ring_flat[:, bass.ds(at, H)], hot(s), parts[:, part, :], start=False,
                                                stop=(part == 2), skip_group_check=True)
                last.then_inc(gathered, 1)

            def step(b, u):
                main = exists(b)
                if main:
                    pe.wait_ge(counts_ready, 1)
                    base, n = chunks_before(nc.tensor, b), chunks_of(nc.tensor, b)
                    at = places(nc.tensor, base)
                if exists(b - 3):
                    pe.wait_ge(aggT_ready, b - 2)
                    nc.tensor.matmul(out2_ps, aggT[:, :], w3t[:, :], start=True, stop=True).then_inc(out2_sums, 1)
                for i in range(STATIC):
                    if i == 2 and exists(b + 1):
                        pe.wait_ge(h1T_ready, b + 2)
                        nc.tensor.matmul(pq_ps, h1T[:, :], w_pq[:, :], start=True, stop=True).then_inc(pq_sums, 1)
                    if i == 2 and exists(b - 1):
                        pe.wait_ge(hm_ready, b)
                        if exists(b - 3):
                            pe.wait_ge(y_ready, b - 2)
                        nc.tensor.transpose(post[:, 0:N], hm[:, 0:N], consts[:, 1, :])
                        nc.tensor.transpose(post[0:H2, N:2 * N], hm[:, N:H], consts[:, 1, :]).then_inc(hmT_sums, 1)
                    if i == 4 and exists(b - 1):
                        pe.wait_ge(hmT_ready, b)
                        nc.tensor.matmul(out1_ps, hmT[:, 0, :], w2a[:, :], start=True, stop=False)
                        nc.tensor.matmul(out1_ps, hmT[0:H2, 1, :], w2b[:, :], start=False, stop=True).then_inc(out1_sums, 1)
                    if i == 5 and exists(b + 2):
                        if exists(b + 1):
                            pe.wait_ge(rest_ready, b + 2)
                        wait_apart(pe, h1_ready, b + 3)
                        nc.tensor.transpose(h1T_ps, h1[:, :], consts[:, 1, :]).then_inc(h1T_sums, 1)
                    if i == 5 and exists(b - 2):
                        pe.wait_ge(h2_ready, b - 1)
                        if exists(b - 1):
                            pe.wait_ge(x1_ready, b)
                        else:
                            pe.wait_ge(y_ready, b - 2)
                        nc.tensor.matmul(aggT_ps, h2[:, :], adj_all[:, b - 2, :], start=True, stop=True).then_inc(aggT_sums, 1)
                    if not main:
                        continue
                    if i == 0:
                        pe.wait_ge(q_ready, b + 1)

                    def chunk(i=i):
                        if u % 2 == 0:
                            pe.wait_ge(onehot_ready, (b - u % 2) // 2 * STATIC + i + 1)
                        gather(base + i, at[i % RING], Q[:, u % 2],
                               lambda s: onehot[:, u // 2 % 2, i * SLOTS + s, u % 2, :])
                    if i < ALWAYS:
                        chunk()
                    else:
                        with pe.If(n > i):
                            chunk()
                if main:
                    with pe.If(n > STATIC):
                        first = loops_before(nc.tensor, b)
                        with pe.Fori(STATIC, n) as i:
                            pe.wait_ge(onehot_loop_ready, first + i - STATIC + 1)
                            gather(base + i, ((base + i) % RING) * STRIDE, Q[:, u % 2], lambda s: onehot_loop[:, s, :])

            graphs(nc.tensor, step)

        @block.scalar
        def _(act):
            act.wait_ge(deg_sums, PARTS)
            nc.scalar.copy(deg[:, :], prep[:, 0:B]).then_inc(deg_ready, 1)
            act.wait_ge(norm1_ready, 1)

            def step(b, u):
                main = exists(b)
                if main:
                    act.wait_ge(counts_ready, 1)
                    base, n = chunks_before(nc.scalar, b), chunks_of(nc.scalar, b)
                    at = places(nc.scalar, base)

                def seed(c, to):
                    wait_apart(act, ring_free, c + 1)
                    dst = ring_flat[:, bass.ds(to, STRIDE)].rearrange("p (a b) -> p a b", a=BANKS)[:, :, 0:ROW]
                    dst = dst.rearrange("p a (s h) -> p a s h", h=H)
                    src = P[:, u % 2, :].unsqueeze(1).unsqueeze(1).broadcast_to([N, BANKS, PER_BANK, H])
                    nc.scalar.copy(dst, src).then_inc(seeded, 1)

                if exists(b - 3):
                    act.wait_ge(aggT_sums, b - 2)
                    if exists(b - 4):
                        act.wait_ge(out2_sums, b - 3)
                    nc.scalar.copy(aggT[:, :], aggT_ps).then_inc(aggT_ready, 1)
                for i in range(STATIC):
                    if i == 1 and exists(b + 1):
                        act.wait_ge(h1T_sums, b + 2)
                        if exists(b):
                            act.wait_ge(pq_sums, b + 1)
                        nc.scalar.copy(h1T[0:F, :], h1T_ps).then_inc(h1T_ready, 1)
                    if i == 2 and exists(b + 2):
                        if exists(b + 1):
                            act.wait_ge(h1T_sums, b + 2)
                        nc.scalar.activation(h1[:, :], x_all[:, b + 2, :], ACT.Relu, bias=shift1[:, bass.ds(b + 2, 1)],
                                             scale=rstd1[:, bass.ds(b + 2, 1)]).then_inc(h1_ready, 1)
                    if i == 4 and exists(b - 1):
                        act.wait_ge(hmT_sums, b)
                        if exists(b - 2):
                            act.wait_ge(out1_sums, b - 1)
                        nc.scalar.copy(hmT[:, 0, :], hmT_ps[:, 0:N])
                        nc.scalar.copy(hmT[0:H2, 1, :], hmT_ps[0:H2, N:2 * N]).then_inc(hmT_ready, 1)
                    if i == 4 and exists(b + 1):
                        act.wait_ge(pq_sums, b + 2)
                        nc.scalar.copy(P[:, (u + 1) % 2, :], pq_ps[:, 0:H])
                        nc.scalar.copy(Q[:, (u + 1) % 2, 0, :], pq_ps[:, H:2 * H]).then_inc(p_ready, 1)
                    if i == 4 and exists(b - 2):
                        act.wait_ge(norm2_ready, b - 1)
                        if exists(b - 3):
                            act.wait_ge(aggT_sums, b - 2)
                        nc.scalar.activation(h2[:, :], x_all[:, b - 2, :], ACT.Relu, bias=shift2[:, u % 2:u % 2 + 1],
                                             scale=rstd2[:, u % 2:u % 2 + 1]).then_inc(h2_ready, 1)
                    if not main:
                        continue
                    if i == 0:
                        act.wait_ge(p_ready, b + 1)
                    if i < ALWAYS:
                        seed(base + i, at[i % RING])
                    else:
                        with act.If(n > i):
                            seed(base + i, at[i % RING])
                if main:
                    with act.If(n > STATIC):
                        with act.Fori(STATIC, n) as i:
                            seed(base + i, ((base + i) % RING) * STRIDE)

            graphs(nc.scalar, step)

        @block.vector
        def _(dve):
            done = [0]

            def chain(ins):
                done[0] += 1
                ins.then_inc(dve_step, 1)
                dve.wait_ge(dve_step, done[0])

            nc.vector.memset(ones[:, :], 1.0)
            for q in range(PER_PART // 4):
                nc.vector.memset(start[:, q // BANKS, q % BANKS, :], 0.0).then_inc(rank_ready, 1)
            nc.vector.memset(half_power[:, :], -0.5)
            nc.vector.memset(h1T[F:F + 1, :], 1.0)
            nc.vector.memset(w_pq[F:F + 1, H:2 * H], 0.0)
            dve.wait_ge(consts_in, 16 * N_CONSTS)
            nc.vector.tensor_scalar(w_pq[0:F, H:2 * H], w1b[:, :], -1.0, None, ALU.mult)
            nc.vector.tensor_tensor(w_pq[0:F, 0:H], w_pq[0:F, 0:H], w1b[:, :], ALU.add)
            nc.vector.tensor_tensor(upto[:, :], consts[:, 0, :], consts[:, 1, :], ALU.add).then_inc(weights_ready, 1)
            dve.wait_ge(x_in, 16)
            with nc.vector.Fori(0, B // 8) as t:
                for i in range(8):
                    last = nc.vector.bn_stats(stats1[:, t * 8 + i, :], x_all[:, t * 8 + i, :])
                last.then_inc(moments_ready, 1)
            dve.wait_ge(moments_ready, B // 8)
            m_even, m_odd, s_even, s_odd = (stats1[:, :, k] for k in (1, 4, 2, 5))
            nc.vector.tensor_tensor(mom[:, 0, :], m_even, m_odd, ALU.add)
            nc.vector.tensor_tensor(mom[:, 1, :], m_even, m_odd, ALU.subtract)
            chain(nc.vector.tensor_tensor(mom[:, 2, :], s_even, s_odd, ALU.add))
            nc.vector.tensor_scalar(mom[:, 0, :], mom[:, 0, :], 0.5, None, ALU.mult)
            nc.vector.tensor_scalar(mom[:, 2, :], mom[:, 2, :], 1.0 / F, EPS, ALU.mult, ALU.add)
            chain(nc.vector.scalar_tensor_tensor(mom[:, 3, :], mom[:, 1, :], 0.25, mom[:, 1, :], ALU.mult, ALU.mult))
            nc.vector.tensor_tensor(mom[:, 3, :], mom[:, 3, :], mom[:, 2, :], ALU.add).then_inc(moments_ready, 1)
            for g in range(PARTS):
                b = slice(g * PER_PART, (g + 1) * PER_PART)
                dve.wait_ge(adj_in[g], 16)
                nc.vector.tensor_scalar(mask_all[:, b, :], adj_all[:, b, :], 0.0, None, ALU.is_gt).then_inc(mask_ready, 1)
            dve.wait_ge(mask_ready, PARTS)
            with nc.vector.Fori(0, PARTS) as g:
                dve.wait_ge(deg_sums, g + 1)
                for q in range(PER_PART // 4):
                    group = g * (PER_PART // 4) + q
                    dve.wait_ge(rank_sums, group + 1)
                    nc.vector.tensor_tensor(rank_all[:, bass.ds(4 * group, 4), :],
                                            ring[:, q, :].rearrange("p (b j) -> p b j", b=4),
                                            mask_all[:, bass.ds(4 * group, 4), :], ALU.mult).then_inc(rank_ready, 1)
            dve.wait_ge(rank_ready, B // 4 + PER_PART // 4)
            dve.wait_ge(degT_ready, 1)
            chain(nc.vector.tensor_reduce(cnt[:, 0:1], post[:, 0:N], AX_X, ALU.max))
            chain(nc.vector.tensor_scalar(cnt_i[:, 0:1], cnt[:, 0:1], float(SLOTS - 1), None, ALU.add))
            chain(nc.vector.tensor_scalar(cnt_i[:, 1:2], cnt_i[:, 0:1], SLOTS.bit_length() - 1, None, ALU.arith_shift_right))
            chain(nc.vector.tensor_scalar(cnt[:, 1:2], cnt_i[:, 1:2], float(ALWAYS), None, ALU.max))
            chain(nc.vector.tensor_scalar(cnt[:, 2:3], cnt[:, 1:2], -float(STATIC), 0.0, ALU.add, ALU.max))
            nc.vector.tensor_scalar(cnt_rows[:, 0, :], consts[:, 0, :], 0.0, cnt[:, 1:2], ALU.mult, ALU.add)
            nc.vector.tensor_scalar(cnt_rows[:, 1, :], consts[:, 0, :], 0.0, cnt[:, 2:3], ALU.mult, ALU.add).then_inc(chunk_counts, 1)
            dve.wait_ge(count_sums, 1)
            nc.vector.tensor_copy(counts[0:1, :, :].rearrange("p a b -> p (a b)"), post[0:1, 0:3 * B]).then_inc(counts_ready, 1)
            chain(nc.vector.scalar_tensor_tensor(spare[:, :], post[:, N:2 * N], -float(SLOTS), deg[:, :], ALU.mult, ALU.add))
            for r in range(RING):
                nc.vector.memset(cnt[:, 3 + r:4 + r], 0.0).then_inc(ring_free, 1)
            dve.wait_ge(counts_ready, 1)

            def hot(pair, u, i):
                for s in range(SLOTS):
                    last = nc.vector.tensor_scalar(onehot[:, u // 2 % 2, i * SLOTS + s, :, :],
                                                   rank_all[:, bass.ds(2 * pair, 2), :], float(i * SLOTS + s + 1), None, ALU.is_equal)
                last.then_inc(onehot_ready, 1)

            def step(b, u):
                main = exists(b)
                if main:
                    base, n = chunks_before(nc.vector, b), chunks_of(nc.vector, b)
                    at = places(nc.vector, base)

                def consume(c, to, first):
                    dve.wait_ge(gathered, c + 1)
                    dve.wait_ge(ring_free, c + RING)
                    src = ring_flat[:, bass.ds(to, STRIDE)].rearrange("p (a b) -> p a b", a=BANKS)[:, :, 0:ROW]
                    nc.vector.scalar_tensor_tensor(acc[:, u % 2], src, 0.0, (start if first else acc)[:, u % 2],
                                                   ALU.max, ALU.add).then_inc(ring_free, 1)

                if exists(b - 3):
                    dve.wait_ge(out2_sums, b - 2)
                    nc.vector.tensor_tensor(x_all[:, b - 3, :], x_all[:, b - 3, :], out2_ps, ALU.add).then_inc(y_ready, 1)
                for i in range(STATIC):
                    if i == 4 and exists(b + 1):
                        dve.wait_ge(p_ready, b + 2)
                        if exists(b):
                            dve.wait_ge(q_ready, b + 1)
                        nc.vector.tensor_tensor(q_rest[:, :], pq_ps[:, H:2 * H], Q[:, (u + 1) % 2, 0, :],
                                                ALU.subtract).then_inc(rest_ready, 1)
                    if i == 4 and exists(b - 1):
                        nc.vector.scalar_tensor_tensor(x_all[:, b - 1, :], b2_rows[:, :], deg[:, bass.ds(b - 1, 1)],
                                                       x_all[:, b - 1, :], ALU.mult, ALU.add).then_inc(xb_ready, 1)
                        dve.wait_ge(xb_ready, b)
                        dve.wait_ge(out1_sums, b)
                        nc.vector.tensor_tensor(x_all[:, b - 1, :], x_all[:, b - 1, :], out1_ps, ALU.add).then_inc(x1_ready, 1)
                        wait_apart(dve, x1_ready, b)
                        nc.vector.bn_stats(stats2[:, :], x_all[:, b - 1, :]).then_inc(stats2_ready, 1)
                        wait_apart(dve, stats2_ready, b)
                        nc.vector.bn_aggr(mv[:, (u + 1) % 2, :], stats2[:, :]).then_inc(mv_ready, 1)
                    if i == 5 and exists(b + 1):
                        nc.vector.tensor_scalar(start[:, (u + 1) % 2, 0, 0:H], P[:, (u + 1) % 2, :], 0.0,
                                                spare[:, bass.ds(b + 1, 1)], ALU.max, ALU.mult).then_inc(start_ready, 1)
                    if i in (1, 2, 3, 5) and exists(b - u % 2 + 2):
                        pair = (b - u % 2) // 2 + 1
                        hot(pair, u + 2, (u % 2) * STATIC // 2 + (1, 2, 3, 5).index(i))
                    if not main:
                        continue
                    if i == 0:
                        dve.wait_ge(start_ready, b + 1)
                        if exists(b - 2):
                            dve.wait_ge(half_ready, b - 1)
                    if i < ALWAYS:
                        consume(base + i, at[i % RING], i == 0)
                    else:
                        with dve.If(n > i):
                            consume(base + i, at[i % RING], False)
                if main:
                    with dve.If(n > STATIC):
                        with dve.Fori(STATIC, n) as i:
                            for s in range(SLOTS):
                                last = nc.vector.tensor_scalar(onehot_loop[:, s, :], rank_all[:, b, :],
                                                               consts[:, 2, bass.ds(i * SLOTS + s, 1)], None, ALU.is_equal)
                            last.then_inc(onehot_loop_ready, 1)
                            consume(base + i, ((base + i) % RING) * STRIDE, False)

            graphs(nc.vector, step)

        @block.gpsimd
        def _(pool):
            pool.wait_ge(moments_ready, B // 8 + 1)
            nc.gpsimd.tensor_tensor(rstd1[:, :], mom[:, 3, :], half_power[:, :], ALU.pow).then_inc(pool_step, 1)
            pool.wait_ge(pool_step, 1)
            nc.gpsimd.tensor_tensor(shift1[:, :], mom[:, 0, :], rstd1[:, :], ALU.mult).then_inc(pool_step, 1)
            pool.wait_ge(pool_step, 2)
            nc.gpsimd.tensor_scalar(shift1[:, :], shift1[:, :], -1.0, None, ALU.mult).then_inc(norm1_ready, 1)
            pool.wait_ge(counts_ready, 1)

            def step(b, u):
                if exists(b - 1):
                    end = chunks_before(nc.gpsimd, b - 1) + chunks_of(nc.gpsimd, b - 1)
                    pool.wait_ge(ring_free, end + RING)
                    if exists(b - 2):
                        pool.wait_ge(hm_ready, b - 1)
                    nc.gpsimd.tensor_tensor(half[:, :], acc[:, (u + 1) % 2, 0, :], acc[:, (u + 1) % 2, 1, :],
                                            ALU.add).then_inc(half_ready, 1)
                    pool.wait_ge(half_ready, b)
                    if exists(b - 2):
                        pool.wait_ge(hmT_sums, b - 1)
                    nc.gpsimd.tensor_tensor(hm[:, :], half[:, 0:H], half[:, H:2 * H], ALU.add).then_inc(hm_ready, 1)
                if exists(b + 1):
                    wait_apart(pool, rest_ready, b + 2)
                    nc.gpsimd.tensor_copy(Q[:, (u + 1) % 2, 1, :], q_rest[:, :]).then_inc(mid_ready, 1)
                    pool.wait_ge(mid_ready, b + 2)
                    nc.gpsimd.tensor_tensor(Q[:, (u + 1) % 2, 2, :], q_rest[:, :], Q[:, (u + 1) % 2, 1, :],
                                            ALU.subtract).then_inc(q_ready, 1)
                if exists(b - 1):
                    k = (u + 1) % 2
                    wait_apart(pool, mv_ready, b)
                    nc.gpsimd.tensor_scalar(ve2[:, :], mv[:, k, 1:2], EPS, None, ALU.add).then_inc(ve2_ready, 1)
                    pool.wait_ge(ve2_ready, b)
                    if exists(b - 2):
                        pool.wait_ge(norm2_ready, b - 1)
                    if exists(b - 3):
                        pool.wait_ge(h2_ready, b - 2)
                    nc.gpsimd.tensor_tensor(rstd2[:, k:k + 1], ve2[:, :], half_power[:, 0:1], ALU.pow).then_inc(rstd2_ready, 1)
                    pool.wait_ge(rstd2_ready, b)
                    nc.gpsimd.tensor_tensor(neg2[:, :], mv[:, k, 0:1], rstd2[:, k:k + 1], ALU.mult).then_inc(neg2_ready, 1)
                    wait_apart(pool, neg2_ready, b)
                    nc.gpsimd.tensor_scalar(shift2[:, k:k + 1], neg2[:, :], -1.0, None, ALU.mult).then_inc(norm2_ready, 1)

            graphs(nc.gpsimd, step)


def kernel(x, adj, L0_gnn_W1, L0_gnn_b1, L0_gnn_W2, L0_gnn_b2, L1_gnn_W):
    import numpy as np
    import concourse.bacc as bacc
    from concourse.bass_utils import run_bass_kernel_spmd

    F = x.shape[2]
    N = x.shape[1]
    k = np.arange(N)
    arrays = {
        "x_nbf": np.ascontiguousarray(np.asarray(x).transpose(1, 0, 2)),
        "adj_kbj": np.ascontiguousarray(np.asarray(adj).transpose(2, 0, 1)),
        "w1a": np.ascontiguousarray(np.asarray(L0_gnn_W1)[:F]),
        "w1b": np.ascontiguousarray(np.asarray(L0_gnn_W1)[F:]),
        "b1": np.ascontiguousarray(np.asarray(L0_gnn_b1)[None, :]),
        "w2": np.ascontiguousarray(L0_gnn_W2),
        "b2": np.ascontiguousarray(L0_gnn_b2),
        "w3t": np.ascontiguousarray(np.asarray(L1_gnn_W).T),
        "ident": np.eye(N, dtype=np.float32),
        "before": (k[:, None] < k[None, :]).astype(np.float32),
        "slot_no": np.tile((k + 1).astype(np.float32), (N, 1)),
    }
    nc = bacc.Bacc("TRN2", target_bir_lowering=False, num_devices=1)
    args = [nc.dram_tensor(n + "_dram", a.shape, mybir.dt.from_np(a.dtype), kind="ExternalInput").ap()
            for n, a in arrays.items()]
    out = nc.dram_tensor("out_dram", arrays["x_nbf"].shape, F32, kind="ExternalOutput").ap()
    gnn_kernel(nc, *args, out)
    r = run_bass_kernel_spmd(nc, [{n + "_dram": a for n, a in arrays.items()}], core_ids=[0])
    return np.ascontiguousarray(r.results[0]["out_dram"].transpose(1, 0, 2))
```

```python
from contextlib import ExitStack

import concourse.bass as bass
from concourse import mybir

F32 = mybir.dt.float32
F16 = mybir.dt.float16
I32 = mybir.dt.int32
ALU = mybir.AluOpType
ACT = mybir.ActivationFunctionType
AX_X = mybir.AxisListType.X

EPS = 1e-5
SLOTS = 4
BANKS = 2
PER_BANK = SLOTS // BANKS
RING = 3
REGULAR = 4
CHUNKS = REGULAR + 1
COVERED = REGULAR * SLOTS
PARTS = 8
QUAD = 4
HOT_RING = 6
BODY = 6
STORE = 4


def gnn_kernel(nc, x, adjT, W1a, W1b, b1, W2, b2, W3T, IDENT, BEFORE, COUNT, out):
    N, B, F = x.shape
    H = W1a.shape[1]
    O = W2.shape[1]
    H2 = H - N
    ROW = PER_BANK * H
    PER_PART = B // PARTS
    QUADS = PER_PART // QUAD
    LOOPED = (N - COVERED) // SLOTS
    SHIFT = SLOTS.bit_length() - 1
    assert N == 128 and B == N and F == O and N < H <= 256 and ROW <= 512 and 2 * H + 2 * O <= 512 and 4 * N <= 512
    assert BODY % 2 == 0 and CHUNKS * BODY % RING == 0 and REGULAR * BODY // 2 % HOT_RING == 0 and HOT_RING == REGULAR + 2 and 1 << SHIFT == SLOTS and QUADS + 2 <= RING * BANKS

    with ExitStack() as ctx:
        def sb(name, shape, dt=F32):
            return ctx.enter_context(nc.sbuf_tensor(name, shape, dt))

        def sem(name):
            return ctx.enter_context(nc.semaphore(name))

        x_all = sb("x_all", [N, B, F])
        adj_all = sb("adj_all", [N, B, N])
        mask_all = sb("mask_all", [N, B, N], F16)
        code_kj = mask_all
        code_jk = sb("code_jk", [N, B, N], F16)
        w_pq = sb("w_pq", [F + 1, 2 * H])
        w2a = sb("w2a", [N, O])
        w2b = sb("w2b", [H2, O])
        w3t = sb("w3t", [F, O])
        b2_rows = sb("b2_rows", [N, O])
        ident = sb("ident", [N, N])
        loop_codes = sb("loop_codes", [N, SLOTS])
        to_scale = sb("to_scale", [N, 4])
        to_scale_i = to_scale[:, :].bitcast(I32)
        ones_row = sb("ones_row", [1, N])
        ident_h = sb("ident_h", [N, N], F16)
        count_h = sb("count_h", [N, N], F16)
        back = sb("back", [N, N], F16)
        ones = sb("ones", [N, N])
        half_power = sb("half_power", [N, 1])
        rstd1 = sb("rstd1", [N, B])
        shift1 = sb("shift1", [N, B])
        deg = sb("deg", [N, B])
        loops = sb("loops", [1, 2, B], I32)
        first_row = sb("first_row", [N, B])
        end_row = sb("end_row", [N, B])
        spare = sb("spare", [N, B])
        h1 = sb("h1", [N, 2, F])
        h1T = sb("h1T", [F + 1, N])
        P = sb("P", [N, 2, H])
        PQ = sb("PQ", [N, 2, 2, 2 * H], F16)
        onehot_space = sb("onehot_space", [N, HOT_RING, SLOTS, N])
        onehot = onehot_space[:, :, :, :].bitcast(F16).rearrange("p c s (g n) -> p c s g n", g=2)
        scratch = onehot_space[:, :, :, :].rearrange("p c s n -> p (c s n)")
        stats1 = scratch[:, 0:6 * B].rearrange("p (b k) -> p b k", k=6)
        mom = scratch[:, 6 * B:10 * B].rearrange("p (k b) -> p k b", b=B)
        rows = scratch[:, 10 * B:11 * B]
        fits = scratch[:, 11 * B:12 * B]
        too_many = scratch[:, 12 * B:13 * B]
        edges_i = scratch[:, 13 * B:14 * B].bitcast(I32)
        rows_i = scratch[:, 14 * B:15 * B].bitcast(I32)
        owned = scratch[:, 15 * B:16 * B]
        upto = scratch[:, 16 * B:17 * B]
        before = scratch[:, 17 * B:18 * B]
        count = scratch[:, 18 * B:19 * B]
        w1b = scratch[0:F, 19 * B:19 * B + H]
        coder = scratch[:, 21 * B:22 * B].bitcast(F16)[:, 0:N]
        onehot_row = sb("onehot_row", [N, SLOTS, N], F16)
        owner = sb("owner", [N, N], F16)
        nth = sb("nth", [N, N], F16)
        by_row = sb("by_row", [N, 2, H + N])
        P_row, ownerT = by_row[:, :, 0:H], by_row[:, :, H:H + N]
        code_row = sb("code_row", [N, N], F16)
        start = sb("start", [N, ROW])
        acc = sb("acc", [N, 2, BANKS, ROW])
        relu_row = sb("relu_row", [N, BANKS, ROW])
        hmT = sb("hmT", [N, 2, N])
        bias = sb("bias", [N, F])
        stats2 = sb("stats2", [N, 6])
        mv = sb("mv", [N, 2, 2])
        ve2 = sb("ve2", [N, 1])
        neg2 = sb("neg2", [N, 1])
        rstd2 = sb("rstd2", [N, 2])
        shift2 = sb("shift2", [N, 2])
        h2 = sb("h2", [N, F])
        aggT = sb("aggT", [F, N])

        ring = ctx.enter_context(nc.psum_tensor("ring", [N, RING, BANKS, 512], F32))
        prep = ctx.enter_context(nc.psum_tensor("prep", [N, 512], F32))
        post = ctx.enter_context(nc.psum_tensor("post", [N, 512], F32))
        bank = [ring[:, k // BANKS, k % BANKS, :] for k in range(RING * BANKS)]
        pq_ps, out1_ps, out2_ps = prep[:, 0:2 * H], prep[:, 2 * H:2 * H + O], prep[:, 2 * H + O:2 * H + 2 * O]
        hmT_ps = (post[:, 0:N], post[0:H2, N:2 * N])
        h1T_ps, aggT_ps = post[0:F, 2 * N:3 * N], post[0:F, 3 * N:4 * N]
        code_row_ps, by_row_ps = post[:, 0:N], post[:, N:2 * N + H]

        consts_in = sem("consts_in")
        x_in = sem("x_in")
        adj_in = [sem(f"adj_in{g}") for g in range(PARTS)]
        weights_ready = sem("weights_ready")
        mask_ready = sem("mask_ready")
        codes_summed = sem("codes_summed")
        code_kj_ready = sem("code_kj_ready")
        code_jk_ready = sem("code_jk_ready")
        largest_ready = sem("largest_ready")
        largest_seen = sem("largest_seen")
        rows_counted = sem("rows_counted")
        fits_ready = sem("fits_ready")
        owned_ready = sem("owned_ready")
        owned_sums = sem("owned_sums")
        tables_ready = sem("tables_ready")
        moments_ready = sem("moments_ready")
        norm1_ready = sem("norm1_ready")
        dve_step = sem("dve_step")
        pool_step = sem("pool_step")
        h1_ready = sem("h1_ready")
        transposed = sem("transposed")
        mixed = sem("mixed")
        h1T_ready = sem("h1T_ready")
        p_ready = sem("p_ready")
        pq_ready = sem("pq_ready")
        start_ready = sem("start_ready")
        onehot_ready = sem("onehot_ready")
        from_ready = sem("from_ready")
        owner_ready = sem("owner_ready")
        nth_ready = sem("nth_ready")
        rows_summed = sem("rows_summed")
        rows_ready = sem("rows_ready")
        onehot_row_ready = sem("onehot_row_ready")
        seeded = sem("seeded")
        gathered = sem("gathered")
        summed = sem("summed")
        relu_row_ready = sem("relu_row_ready")
        onehot_loop_ready = sem("onehot_loop_ready")
        loop_codes_ready = sem("loop_codes_ready")
        loop_seeded = sem("loop_seeded")
        loop_gathered = sem("loop_gathered")
        loop_summed = sem("loop_summed")
        half_ready = sem("half_ready")
        hm_ready = sem("hm_ready")
        half_row_ready = sem("half_row_ready")
        hm_row_ready = sem("hm_row_ready")
        hmT_ready = sem("hmT_ready")
        bias_ready = sem("bias_ready")
        xb_ready = sem("xb_ready")
        x1_ready = sem("x1_ready")
        stats2_ready = sem("stats2_ready")
        mv_ready = sem("mv_ready")
        ve2_ready = sem("ve2_ready")
        rstd2_ready = sem("rstd2_ready")
        neg2_ready = sem("neg2_ready")
        norm2_ready = sem("norm2_ready")
        h2_ready = sem("h2_ready")
        aggT_ready = sem("aggT_ready")
        y_ready = sem("y_ready")
        stored = sem("stored")

        HEAD, TAIL = 3, 4
        N_CONSTS = 10

        def graphs(eng, step):
            for b in range(-HEAD, BODY):
                step(b, b % BODY)
            rounds = (B - HEAD) // BODY
            with eng.Fori(1, rounds) as t:
                for u in range(BODY):
                    step(t * BODY + u, u)
            for b in range(rounds * BODY, B + TAIL):
                step(b, b % BODY)

        def exists(b):
            return not isinstance(b, int) or 0 <= b < B

        def place(u, i):
            return (CHUNKS * u + i) % RING

        def hot_place(pair, i):
            return (REGULAR * pair + i) % HOT_RING

        def load(eng, which, b):
            return eng.value_load(loops[0:1, which, bass.ds(b, 1)], min_val=0,
                                  max_val=LOOPED * (1 if which else B))

        def any_loops(eng):
            return eng.snap(load(eng, 0, B - 1) + load(eng, 1, B - 1))

        until = {}
        for eng in (nc.tensor, nc.scalar, nc.vector, nc.gpsimd):
            until[eng.engine] = eng.alloc_register("until")

        def wait_apart(eng, semaphore, value):
            if not isinstance(value, int):
                eng.reg_mov(until[eng.engine], value)
                eng.wait_ge(weights_ready, 1)
                value = until[eng.engine]
            eng.wait_ge(semaphore, value)

        block = ctx.enter_context(nc.Block())

        @block.sync
        def _(sp):
            def load_part(g):
                b = slice(g * PER_PART, (g + 1) * PER_PART)
                sp.dma_start(adj_all[:, b, :], adjT[:, b, :]).then_inc(adj_in[g], 16)

            with nc.allow_non_contiguous_dma("small weights"):
                for dst, src in ((before, BEFORE), (ident[:, :], IDENT), (count, COUNT),
                                 (w_pq[0:F, 0:H], W1a), (w1b, W1b), (w_pq[F:F + 1, 0:H], b1)):
                    sp.dma_start(dst, src).then_inc(consts_in, 16)
                load_part(0)
                for dst, src in ((w2a[:, :], W2[0:N, :]), (w2b[:, :], W2[N:H, :]), (w3t[:, :], W3T),
                                 (b2_rows[:, :], b2.partition_broadcast(N))):
                    sp.dma_start(dst, src).then_inc(consts_in, 16)
            sp.dma_start(x_all[:, :, :], x).then_inc(x_in, 16)
            for g in range(1, PARTS):
                load_part(g)
            with sp.Fori(0, B // STORE) as t:
                sp.wait_ge(y_ready, t * STORE + STORE)
                b = bass.ds(t * STORE, STORE)
                sp.dma_start(out[:, b, :], x_all[:, b, :]).then_inc(stored, 16)
            sp.wait_ge(stored, 16 * B // STORE)

        @block.tensor
        def _(pe):
            def codes(g):
                pe.wait_ge(mask_ready, g + 1)
                for q in range(QUADS):
                    quad = g * QUADS + q
                    later = not isinstance(g, int) or g > 0
                    if later:
                        pe.wait_ge(code_kj_ready, quad - QUADS + 1)
                    nc.tensor.matmul(bank[q], coder, mask_all[:, bass.ds(QUAD * quad, QUAD), :], start=True, stop=True)
                    if q >= 2 or later:
                        pe.wait_ge(code_jk_ready, quad - 2 + 1)
                    for i in range(QUAD):
                        mask = mask_all[:, QUAD * quad + i, :]
                        last = nc.tensor.matmul(bank[QUADS + q % 2][:, i * N:(i + 1) * N], mask, coder, start=True, stop=True)
                    last.then_inc(codes_summed, 1)

            pe.wait_ge(largest_ready, 1)
            nc.tensor.matmul(post[0:1, 0:F + 1], to_scale[0:F + 1, 0:1], ident[0:F + 1, 0:F + 1], start=True,
                             stop=True).then_inc(largest_seen, 1)
            pe.wait_ge(largest_ready, 2)
            nc.tensor.matmul(post[:, N:N + 1], ones_row[:, :], to_scale[0:1, 1:2], start=True, stop=True).then_inc(largest_seen, 1)
            codes(0)
            with pe.Fori(1, PARTS) as g:
                codes(g)
            pe.wait_ge(code_kj_ready, B // QUAD)
            pe.wait_ge(code_jk_ready, B // QUAD)
            for k in range(RING * BANKS):
                nc.tensor.matmul(bank[k], coder, code_jk[:, 0:QUAD, :], start=True, stop=True)
            pe.wait_ge(rows_counted, 1)
            nc.tensor.matmul(post[:, 0:B], ones[:, :], rows, start=True, stop=True)
            nc.tensor.matmul(post[:, N:2 * N], rows, ones[:, :], start=True, stop=True).then_inc(rows_summed, 1)
            pe.wait_ge(owned_ready, 1)
            nc.tensor.matmul(prep[:, 0:B], upto, owned, start=True, stop=True)
            nc.tensor.matmul(prep[:, N:2 * N], too_many, before, start=True, stop=True).then_inc(owned_sums, 1)
            pe.wait_ge(tables_ready, 1)
            some_loops = any_loops(nc.tensor)

            def gather(to, parts, hot):
                for s in range(SLOTS):
                    dst = ring[:, to, s // PER_BANK, s % PER_BANK * H:(s % PER_BANK + 1) * H]
                    for part in range(2):
                        last = nc.tensor.matmul(dst, hot(s), parts[:, part, H:2 * H], start=False, stop=(part == 1),
                                                skip_group_check=True)
                return last

            def step(b, u):
                main = exists(b)
                parts = PQ[:, u % 2]
                for i in range(CHUNKS):
                    if main:
                        if i == 0:
                            pe.wait_ge(pq_ready, b + 1)
                        if i < REGULAR:
                            if u % 2 == 0:
                                pe.wait_ge(onehot_ready, b * (REGULAR // 2) + i + 1)
                            hot = lambda s: onehot[:, hot_place(u // 2, i), s, u % 2, :]
                        else:
                            pe.wait_ge(onehot_row_ready, b + 1)
                            hot = lambda s: onehot_row[:, s, :]
                        pe.wait_ge(seeded, b * CHUNKS + i + 1)
                        gather(place(u, i), parts, hot).then_inc(gathered, 1)
                    if i == 0 and main:
                        pe.wait_ge(nth_ready, b + 1)
                        if exists(b - 4):
                            pe.wait_ge(aggT_ready, b - 3)
                        elif exists(b - 2):
                            pe.wait_ge(hmT_ready, b - 1)
                        else:
                            pe.wait_ge(h1T_ready, b + 2)
                        nc.tensor.matmul(code_row_ps, code_jk[:, b, :], owner[:, :], start=True, stop=False)
                        nc.tensor.matmul(code_row_ps, back[:, :], nth[:, :], start=False, stop=True)
                        for part in range(2):
                            nc.tensor.matmul(by_row_ps[:, 0:H], owner[:, :], parts[:, part, 0:H], start=(part == 0), stop=(part == 1))
                        nc.tensor.matmul(by_row_ps[:, H:H + N], owner[:, :], ident_h[:, :], start=True,
                                         stop=True).then_inc(rows_summed, 1)
                    if i == 1:
                        if exists(b - 5):
                            pe.wait_ge(y_ready, b - 4)
                        elif exists(b):
                            pe.wait_ge(pq_ready, b + 1)
                        if exists(b + 1):
                            pe.wait_ge(h1T_ready, b + 2)
                            last = nc.tensor.matmul(pq_ps, h1T[:, :], w_pq[:, :], start=True, stop=True)
                        if exists(b - 2):
                            pe.wait_ge(hmT_ready, b - 1)
                            nc.tensor.matmul(out1_ps, hmT[:, 0, :], w2a[:, :], start=True, stop=False)
                            last = nc.tensor.matmul(out1_ps, hmT[0:H2, 1, :], w2b[:, :], start=False, stop=True)
                        if exists(b - 4):
                            pe.wait_ge(aggT_ready, b - 3)
                            last = nc.tensor.matmul(out2_ps, aggT[:, :], w3t[:, :], start=True, stop=True)
                        if exists(b + 1) or exists(b - 2) or exists(b - 4):
                            last.then_inc(mixed, 1)
                    if i == 3:
                        if main:
                            pe.wait_ge(rows_ready, b + 1)
                        if exists(b + 2):
                            pe.wait_ge(h1_ready, b + 3)
                            last = nc.tensor.matmul(h1T_ps, h1[:, u % 2, :], ident[:, :], start=True, stop=True)
                        if exists(b - 1):
                            pe.wait_ge(hm_ready, b)
                            pe.wait_ge(hm_row_ready, b)
                            hm, hm_row = acc[:, (u + 1) % 2, 0, 0:H], relu_row[:, 0, 0:H]
                            for k, h in enumerate((slice(0, N), slice(N, H))):
                                nc.tensor.matmul(hmT_ps[k], hm[:, h], ident[:, :], start=True, stop=False)
                                last = nc.tensor.matmul(hmT_ps[k], hm_row[:, h], ownerT[:, (u + 1) % 2, :], start=False, stop=True)
                        if exists(b - 3):
                            pe.wait_ge(h2_ready, b - 2)
                            last = nc.tensor.matmul(aggT_ps, h2[:, :], adj_all[:, b - 3, :], start=True, stop=True)
                        if exists(b + 2) or exists(b - 1) or exists(b - 3):
                            last.then_inc(transposed, 1)
                if main:
                    with nc.tensor.If(some_loops > 0):
                        first, n = load(nc.tensor, 0, b), load(nc.tensor, 1, b)
                        with nc.tensor.If(n > 0):
                            with nc.tensor.Fori(0, n) as k:
                                pe.wait_ge(onehot_loop_ready, first + k + 1)
                                pe.wait_ge(loop_seeded, first + k + 1)
                                gather(place(u, CHUNKS), parts, lambda s: onehot_row[:, s, :]).then_inc(loop_gathered, 1)

            graphs(nc.tensor, step)

        @block.scalar
        def _(act):
            def codes(g):
                for q in range(QUADS):
                    quad = g * QUADS + q
                    b = bass.ds(QUAD * quad, QUAD)
                    wait_apart(act, codes_summed, quad + 1)
                    nc.scalar.copy(code_kj[:, b, :], bank[q].rearrange("p (b j) -> p b j", b=QUAD)).then_inc(code_kj_ready, 1)
                    nc.scalar.copy(code_jk[:, b, :], bank[QUADS + q % 2].rearrange("p (b k) -> p b k", b=QUAD)).then_inc(code_jk_ready, 1)

            codes(0)
            with nc.scalar.Fori(1, PARTS) as g:
                codes(g)
            act.wait_ge(norm1_ready, 1)
            act.wait_ge(tables_ready, 1)
            some_loops = any_loops(nc.scalar)

            def seed(to, src):
                dst = ring[:, to, :, 0:ROW].rearrange("p a (s h) -> p a s h", h=H)
                return nc.scalar.copy(dst, src.unsqueeze(1).unsqueeze(1).broadcast_to([N, BANKS, PER_BANK, H]))

            def step(b, u):
                main = exists(b)
                for i in range(CHUNKS):
                    if main:
                        if i == 0:
                            act.wait_ge(p_ready, b + 1)
                        if i in (0, 1) and exists(b - 1):
                            act.wait_ge(summed, b * REGULAR - 1 + i)
                        if i == 2 and exists(b - 1):
                            act.wait_ge(relu_row_ready, b)
                        if i in (3, 4):
                            act.wait_ge(summed, b * REGULAR + i - 2)
                        if i == 4:
                            act.wait_ge(rows_ready, b + 1)
                        seed(place(u, i), P[:, u % 2, :] if i < REGULAR else P_row[:, u % 2, :]).then_inc(seeded, 1)
                    if i == 0 and exists(b + 1):
                        act.wait_ge(transposed, b + 2)
                        if main:
                            act.wait_ge(mixed, b + 1)
                        nc.scalar.copy(h1T[0:F, :], h1T_ps).then_inc(h1T_ready, 1)
                    if i == 0 and exists(b - 2):
                        act.wait_ge(transposed, b + 2)
                        if exists(b - 3):
                            act.wait_ge(mixed, b + 1)
                        nc.scalar.copy(hmT[:, 0, :], hmT_ps[0])
                        nc.scalar.copy(hmT[0:H2, 1, :], hmT_ps[1]).then_inc(hmT_ready, 1)
                    if i == 0 and exists(b - 4):
                        act.wait_ge(transposed, b + 2)
                        if exists(b - 5):
                            act.wait_ge(mixed, b + 1)
                        nc.scalar.copy(aggT[:, :], aggT_ps).then_inc(aggT_ready, 1)
                    if i == 1 and exists(b - 1):
                        act.wait_ge(gathered, b * CHUNKS)
                        if exists(b - 2):
                            act.wait_ge(transposed, b + 2)
                        nc.scalar.activation(relu_row[:, :, :], ring[:, place(u, -1), :, 0:ROW], ACT.Relu).then_inc(relu_row_ready, 1)
                    if i == 2 and main:
                        act.wait_ge(rows_summed, b + 2)
                        if exists(b - 1):
                            act.wait_ge(onehot_row_ready, b)
                        nc.scalar.copy(code_row[:, :], code_row_ps)
                        if exists(b - 2):
                            act.wait_ge(transposed, b + 2)
                        nc.scalar.copy(by_row[:, u % 2, :], by_row_ps).then_inc(rows_ready, 1)
                    if i == 3 and exists(b + 1):
                        act.wait_ge(mixed, b + 2)
                        if exists(b - 1):
                            act.wait_ge(gathered, b * CHUNKS)
                        nc.scalar.copy(PQ[:, (u + 1) % 2, 0, :], pq_ps)
                        if exists(b - 1):
                            act.wait_ge(start_ready, b)
                        nc.scalar.copy(P[:, (u + 1) % 2, :], pq_ps[:, 0:H]).then_inc(p_ready, 1)
                    if i == 3 and exists(b - 3):
                        k = (u + 1) % 2
                        wait_apart(act, norm2_ready, b - 2)
                        if exists(b - 4):
                            act.wait_ge(transposed, b + 2)
                        nc.scalar.activation(h2[:, :], x_all[:, b - 3, :], ACT.Relu, bias=shift2[:, k:k + 1],
                                             scale=rstd2[:, k:k + 1]).then_inc(h2_ready, 1)
                    if i == 4 and exists(b + 3):
                        if exists(b + 1):
                            act.wait_ge(transposed, b + 2)
                        nc.scalar.activation(h1[:, (u + 1) % 2, :], x_all[:, b + 3, :], ACT.Relu, bias=shift1[:, bass.ds(b + 3, 1)],
                                             scale=rstd1[:, bass.ds(b + 3, 1)]).then_inc(h1_ready, 1)
                if main:
                    with nc.scalar.If(some_loops > 0):
                        first, n = load(nc.scalar, 0, b), load(nc.scalar, 1, b)
                        with nc.scalar.If(n > 0):
                            act.wait_ge(summed, b * REGULAR + 3)
                            with nc.scalar.Fori(0, n) as k:
                                wait_apart(act, loop_summed, first + k + 1)
                                seed(place(u, CHUNKS), P[:, u % 2, :]).then_inc(loop_seeded, 1)
                            wait_apart(act, loop_summed, first + n + 1)
                            act.reg_mov(until[act.engine], first + n)

            graphs(nc.scalar, step)

        @block.vector
        def _(dve):
            done = [0]

            def chain(ins):
                done[0] += 1
                ins.then_inc(dve_step, 1)
                dve.wait_ge(dve_step, done[0])

            nc.vector.memset(ones[:, :], 1.0)
            nc.vector.memset(ones_row[:, :], 1.0)
            nc.vector.memset(half_power[:, :], -0.5)
            nc.vector.memset(back[:, :], -2.0 * SLOTS)
            nc.vector.memset(start[:, :], 0.0)
            nc.vector.memset(h1T[F:F + 1, :], 1.0).then_inc(loop_summed, 1)
            nc.vector.memset(w_pq[F:F + 1, H:2 * H], 0.0)
            dve.wait_ge(consts_in, 16 * N_CONSTS)
            nc.vector.tensor_scalar(w_pq[0:F, H:2 * H], w1b, -1.0, None, ALU.mult)
            nc.vector.tensor_tensor(w_pq[0:F, 0:H], w_pq[0:F, 0:H], w1b, ALU.add)
            nc.vector.tensor_tensor(upto, before, ident[:, :], ALU.add)
            nc.vector.scalar_tensor_tensor(coder, before, 2.0, ident[:, :], ALU.mult, ALU.add)
            nc.vector.tensor_scalar(count_h[:, :], count, 1.0, None, ALU.mult)
            nc.vector.tensor_scalar(ident_h[:, :], ident[:, :], 1.0, None, ALU.mult).then_inc(weights_ready, 1)
            dve.wait_ge(weights_ready, 1)
            nc.vector.tensor_reduce(to_scale[0:F + 1, 0:1], w_pq[:, :], AX_X, ALU.max, apply_absolute_value=True).then_inc(largest_ready, 1)
            dve.wait_ge(largest_seen, 1)
            nc.vector.tensor_reduce(to_scale[0:1, 1:2], post[0:1, 0:F + 1], AX_X, ALU.max).then_inc(largest_ready, 1)
            dve.wait_ge(largest_seen, 2)
            chain(nc.vector.tensor_copy(to_scale[:, 2:3], post[:, N:N + 1]))
            exponent = 1 << 23
            chain(nc.vector.tensor_scalar(to_scale_i[:, 3:4], to_scale_i[:, 2:3], 255 * exponent, None, ALU.bitwise_and))
            chain(nc.vector.tensor_scalar(to_scale_i[:, 3:4], to_scale_i[:, 3:4], float((127 - 100) * exponent), None, ALU.max))
            nc.vector.tensor_scalar(to_scale_i[:, 2:3], to_scale_i[:, 3:4], -1.0, float((2 * 127 + 8) * exponent), ALU.mult, ALU.add)
            chain(nc.vector.tensor_scalar(to_scale_i[:, 3:4], to_scale_i[:, 3:4], float(-8 * exponent), None, ALU.add))
            nc.vector.tensor_scalar(w_pq[:, :], w_pq[:, :], to_scale[0:F + 1, 2:3], None, ALU.mult)
            nc.vector.tensor_scalar(w2a[:, :], w2a[:, :], to_scale[:, 3:4], None, ALU.mult)
            nc.vector.tensor_scalar(w2b[:, :], w2b[:, :], to_scale[0:H2, 3:4], None, ALU.mult).then_inc(weights_ready, 1)

            for g in range(PARTS):
                b = slice(g * PER_PART, (g + 1) * PER_PART)
                dve.wait_ge(adj_in[g], 16)
                nc.vector.tensor_scalar(mask_all[:, b, :], adj_all[:, b, :], 0.0, None, ALU.is_gt).then_inc(mask_ready, 1)
                if g == 0:
                    dve.wait_ge(x_in, 16)
                with nc.vector.Fori(0, QUADS) as q:
                    for i in range(QUAD):
                        b = g * PER_PART + q * QUAD + i
                        last = nc.vector.bn_stats(stats1[:, b, :], x_all[:, b, :])
                    last.then_inc(moments_ready, 1)
            dve.wait_ge(moments_ready, B // QUAD)
            m_even, m_odd, s_even, s_odd = (stats1[:, :, k] for k in (1, 4, 2, 5))
            nc.vector.tensor_tensor(mom[:, 0, :], m_even, m_odd, ALU.add)
            nc.vector.tensor_tensor(mom[:, 1, :], m_even, m_odd, ALU.subtract)
            chain(nc.vector.tensor_tensor(mom[:, 2, :], s_even, s_odd, ALU.add))
            nc.vector.tensor_scalar(mom[:, 0, :], mom[:, 0, :], 0.5, None, ALU.mult)
            nc.vector.tensor_scalar(mom[:, 2, :], mom[:, 2, :], 1.0 / F, EPS, ALU.mult, ALU.add)
            chain(nc.vector.scalar_tensor_tensor(mom[:, 3, :], mom[:, 1, :], 0.25, mom[:, 1, :], ALU.mult, ALU.mult))
            nc.vector.tensor_tensor(mom[:, 3, :], mom[:, 3, :], mom[:, 2, :], ALU.add).then_inc(moments_ready, 1)

            dve.wait_ge(code_jk_ready, B // QUAD)
            chain(nc.vector.tensor_scalar(edges_i, code_jk[:, :, N - 1], 1.0, None, ALU.add))
            chain(nc.vector.tensor_scalar(edges_i, edges_i, 1, None, ALU.arith_shift_right))
            nc.vector.tensor_copy(deg[:, :], edges_i)
            chain(nc.vector.tensor_scalar(rows_i, edges_i, float(SLOTS - 1 - COVERED), 0.0, ALU.add, ALU.max))
            chain(nc.vector.tensor_scalar(rows_i, rows_i, SHIFT, None, ALU.arith_shift_right))
            nc.vector.tensor_copy(rows, rows_i).then_inc(rows_counted, 1)
            dve.wait_ge(rows_summed, 1)
            dve.wait_ge(rows_counted, 1)
            chain(nc.vector.tensor_scalar(fits, post[:, 0:B], float(N), None, ALU.is_le))
            nc.vector.tensor_scalar(too_many, post[:, N:2 * N], float(N), None, ALU.is_gt)
            nc.vector.tensor_tensor(owned, rows, fits, ALU.mult).then_inc(owned_ready, 1)
            dve.wait_ge(owned_ready, 1)
            chain(nc.vector.scalar_tensor_tensor(spare[:, :], owned, -float(SLOTS), deg[:, :], ALU.mult, ALU.add))
            chain(nc.vector.scalar_tensor_tensor(spare[:, :], fits, float(SLOTS * LOOPED), spare[:, :], ALU.mult, ALU.add))
            chain(nc.vector.tensor_scalar(spare[:, :], spare[:, :], -float(COVERED + SLOTS * LOOPED), 1.0 / BANKS, ALU.add, ALU.mult))
            nc.vector.tensor_scalar(loops[0:1, 1, :], fits[0:1, :], -float(LOOPED), float(LOOPED), ALU.mult, ALU.add)
            dve.wait_ge(owned_sums, 1)
            nc.vector.tensor_scalar(loops[0:1, 0, :], prep[0:1, N:2 * N], float(LOOPED), None, ALU.mult)
            nc.vector.tensor_copy(end_row[:, :], prep[:, 0:B])
            nc.vector.tensor_tensor(first_row[:, :], prep[:, 0:B], owned, ALU.subtract).then_inc(tables_ready, 1)
            dve.wait_ge(tables_ready, 1)
            dve.wait_ge(norm1_ready, 1)
            some_loops = any_loops(nc.vector)

            def hot(pair, u, i, s):
                return nc.vector.tensor_scalar(onehot[:, hot_place(u // 2, i), s, :, :], code_kj[:, bass.ds(2 * pair, 2), :],
                                               2.0 * (SLOTS * i + s) + 1.0, None, ALU.is_equal)

            def consume(u, to, first):
                so_far = start[:, :].unsqueeze(1).broadcast_to([N, BANKS, ROW]) if first else acc[:, u % 2]
                return nc.vector.scalar_tensor_tensor(acc[:, u % 2], ring[:, to, :, 0:ROW], 0.0, so_far, ALU.max, ALU.add)

            def step(b, u):
                main = exists(b)
                at = bass.ds(b + 1, 1)
                for i in range(CHUNKS):
                    k = i if u % 2 == 0 else i - 1 + REGULAR
                    if (i > 0 if u % 2 else i < REGULAR) and exists(b - u % 2 + 2):
                        for s in range(k % 2 * 2, k % 2 * 2 + 2):
                            last = hot((b - u % 2) // 2 + 1, u - u % 2 + 2, k // 2, s)
                        if k % 2:
                            last.then_inc(onehot_ready, 1)
                    if main and i < REGULAR:
                        if i == 0:
                            dve.wait_ge(start_ready, b + 1)
                            if exists(b - 2):
                                dve.wait_ge(transposed, b + 2)
                        else:
                            dve.wait_ge(summed, b * REGULAR + i)
                        dve.wait_ge(gathered, b * CHUNKS + i + 1)
                        consume(u, place(u, i), i == 0).then_inc(summed, 1)
                    if i == 0 and exists(b + 1):
                        if main:
                            dve.wait_ge(rows_summed, b + 2)
                        nc.vector.tensor_scalar(nth[:, :], count_h[:, :], first_row[:, at], None, ALU.is_ge).then_inc(from_ready, 1)
                    if i == 1 and exists(b + 1):
                        dve.wait_ge(from_ready, b + 2)
                        nc.vector.scalar_tensor_tensor(owner[:, :], count_h[:, :], end_row[:, at], nth[:, :], ALU.is_lt,
                                                       ALU.mult).then_inc(owner_ready, 1)
                    if i == 2 and exists(b + 1):
                        dve.wait_ge(owner_ready, b + 2)
                        nc.vector.scalar_tensor_tensor(nth[:, :], count_h[:, :], first_row[:, at], owner[:, :], ALU.subtract,
                                                       ALU.mult).then_inc(nth_ready, 1)
                    if i == 2 and main:
                        dve.wait_ge(rows_ready, b + 1)
                        for s in range(SLOTS):
                            last = nc.vector.tensor_scalar(onehot_row[:, s, :], code_row[:, :], 2.0 * (COVERED + s) + 1.0, None,
                                                           ALU.is_equal)
                        last.then_inc(onehot_row_ready, 1)
                    if i == 3 and exists(b - 2):
                        dve.wait_ge(xb_ready, b - 1)
                        dve.wait_ge(mixed, b + 2)
                        if exists(b + 1):
                            dve.wait_ge(p_ready, b + 2)
                        nc.vector.tensor_tensor(x_all[:, b - 2, :], x_all[:, b - 2, :], out1_ps, ALU.add).then_inc(x1_ready, 1)
                    if i == 3 and exists(b + 1):
                        dve.wait_ge(p_ready, b + 2)
                        nc.vector.tensor_tensor(PQ[:, (u + 1) % 2, 1, :], pq_ps, PQ[:, (u + 1) % 2, 0, :],
                                                ALU.subtract).then_inc(pq_ready, 1)
                    if i == 3 and exists(b - 2):
                        wait_apart(dve, x1_ready, b - 1)
                        nc.vector.bn_stats(stats2[:, :], x_all[:, b - 2, :]).then_inc(stats2_ready, 1)
                    if i == 4 and exists(b - 4):
                        dve.wait_ge(mixed, b + 2)
                        nc.vector.tensor_tensor(x_all[:, b - 4, :], x_all[:, b - 4, :], out2_ps, ALU.add).then_inc(y_ready, 1)
                    if i == 4 and exists(b - 2):
                        wait_apart(dve, stats2_ready, b - 1)
                        nc.vector.bn_aggr(mv[:, u % 2, :], stats2[:, :]).then_inc(mv_ready, 1)
                    if i == 4 and exists(b + 1):
                        dve.wait_ge(p_ready, b + 2)
                        nc.vector.tensor_scalar(start[:, 0:H], P[:, (u + 1) % 2, :], 0.0, spare[:, at], ALU.max,
                                                ALU.mult).then_inc(start_ready, 1)
                if main:
                    with nc.vector.If(some_loops > 0):
                        first, n = load(nc.vector, 0, b), load(nc.vector, 1, b)
                        with nc.vector.If(n > 0):
                            with nc.vector.Fori(0, n) as k:
                                edges = bass.ds(k * SLOTS + COVERED, SLOTS)
                                wait_apart(dve, summed, b * REGULAR + REGULAR)
                                dve.wait_ge(gathered, b * CHUNKS + CHUNKS)
                                nc.vector.tensor_scalar(loop_codes[:, :], count_h[:, edges], 2.0, 1.0, ALU.mult,
                                                        ALU.add).then_inc(loop_codes_ready, 1)
                                wait_apart(dve, loop_codes_ready, first + k + 1)
                                for s in range(SLOTS):
                                    last = nc.vector.tensor_scalar(onehot_row[:, s, :], code_kj[:, b, :],
                                                                   loop_codes[:, s:s + 1], None, ALU.is_equal)
                                last.then_inc(onehot_loop_ready, 1)
                                dve.wait_ge(loop_summed, first + k + 1)
                                dve.wait_ge(loop_gathered, first + k + 1)
                                consume(u, place(u, CHUNKS), False).then_inc(loop_summed, 1)

            graphs(nc.vector, step)

        @block.gpsimd
        def _(pool):
            pool.wait_ge(moments_ready, B // QUAD + 1)
            nc.gpsimd.tensor_tensor(rstd1[:, :], mom[:, 3, :], half_power[:, :].broadcast_to([N, B]), ALU.pow).then_inc(pool_step, 1)
            pool.wait_ge(pool_step, 1)
            nc.gpsimd.tensor_tensor(shift1[:, :], mom[:, 0, :], rstd1[:, :], ALU.mult).then_inc(pool_step, 1)
            pool.wait_ge(pool_step, 2)
            nc.gpsimd.tensor_scalar(shift1[:, :], shift1[:, :], -1.0, None, ALU.mult).then_inc(norm1_ready, 1)
            pool.wait_ge(tables_ready, 1)
            some_loops = any_loops(nc.gpsimd)

            def step(b, u):
                if exists(b - 1):
                    with nc.gpsimd.If(some_loops > 0):
                        pool.wait_ge(loop_summed, load(nc.gpsimd, 0, b - 1) + load(nc.gpsimd, 1, b - 1) + 1)
                    pool.wait_ge(summed, b * REGULAR)
                    half = acc[:, (u + 1) % 2, 0, :]
                    nc.gpsimd.tensor_tensor(half, half, acc[:, (u + 1) % 2, 1, :], ALU.add).then_inc(half_ready, 1)
                    pool.wait_ge(half_ready, b)
                    nc.gpsimd.tensor_tensor(half[:, 0:H], half[:, 0:H], half[:, H:2 * H], ALU.add).then_inc(hm_ready, 1)
                if exists(b - 3):
                    k = (u + 1) % 2
                    wait_apart(pool, mv_ready, b - 2)
                    nc.gpsimd.tensor_scalar(ve2[:, :], mv[:, k, 1:2], EPS, None, ALU.add).then_inc(ve2_ready, 1)
                    pool.wait_ge(ve2_ready, b - 2)
                    if exists(b - 4):
                        pool.wait_ge(norm2_ready, b - 3)
                    if exists(b - 5):
                        pool.wait_ge(h2_ready, b - 4)
                    nc.gpsimd.tensor_tensor(rstd2[:, k:k + 1], ve2[:, :], half_power[:, :], ALU.pow).then_inc(rstd2_ready, 1)
                    pool.wait_ge(rstd2_ready, b - 2)
                    nc.gpsimd.tensor_tensor(neg2[:, :], mv[:, k, 0:1], rstd2[:, k:k + 1], ALU.mult).then_inc(neg2_ready, 1)
                    wait_apart(pool, neg2_ready, b - 2)
                    nc.gpsimd.tensor_scalar(shift2[:, k:k + 1], neg2[:, :], -1.0, None, ALU.mult).then_inc(norm2_ready, 1)
                if exists(b - 1):
                    pool.wait_ge(relu_row_ready, b)
                    half = relu_row[:, 0, :]
                    nc.gpsimd.tensor_tensor(half, half, relu_row[:, 1, :], ALU.add).then_inc(half_row_ready, 1)
                    pool.wait_ge(half_row_ready, b)
                    nc.gpsimd.tensor_tensor(half[:, 0:H], half[:, 0:H], half[:, H:2 * H], ALU.add).then_inc(hm_row_ready, 1)
                if exists(b - 1):
                    wait_apart(pool, h1_ready, b)
                    if exists(b - 2):
                        pool.wait_ge(xb_ready, b - 1)
                    nc.gpsimd.tensor_tensor(bias[:, :], b2_rows[:, :], deg[:, bass.ds(b - 1, 1)].broadcast_to([N, F]),
                                            ALU.mult).then_inc(bias_ready, 1)
                    wait_apart(pool, bias_ready, b)
                    nc.gpsimd.tensor_tensor(x_all[:, b - 1, :], x_all[:, b - 1, :], bias[:, :], ALU.add).then_inc(xb_ready, 1)

            graphs(nc.gpsimd, step)


def kernel(x, adj, L0_gnn_W1, L0_gnn_b1, L0_gnn_W2, L0_gnn_b2, L1_gnn_W):
    import numpy as np
    import concourse.bacc as bacc
    from concourse.bass_utils import run_bass_kernel_spmd

    F = x.shape[2]
    N = x.shape[1]
    k = np.arange(N)
    arrays = {
        "x_nbf": np.ascontiguousarray(np.asarray(x).transpose(1, 0, 2)),
        "adj_kbj": np.ascontiguousarray(np.asarray(adj).transpose(2, 0, 1)),
        "w1a": np.ascontiguousarray(np.asarray(L0_gnn_W1)[:F]),
        "w1b": np.ascontiguousarray(np.asarray(L0_gnn_W1)[F:]),
        "b1": np.ascontiguousarray(np.asarray(L0_gnn_b1)[None, :]),
        "w2": np.ascontiguousarray(L0_gnn_W2),
        "b2": np.ascontiguousarray(L0_gnn_b2),
        "w3t": np.ascontiguousarray(np.asarray(L1_gnn_W).T),
        "ident": np.eye(N, dtype=np.float32),
        "before": (k[:, None] < k[None, :]).astype(np.float32),
        "count": np.broadcast_to(k.astype(np.float32), (N, N)).copy(),
    }
    nc = bacc.Bacc("TRN2", target_bir_lowering=False, num_devices=1)
    args = [nc.dram_tensor(n + "_dram", a.shape, mybir.dt.from_np(a.dtype), kind="ExternalInput").ap()
            for n, a in arrays.items()]
    out = nc.dram_tensor("out_dram", arrays["x_nbf"].shape, F32, kind="ExternalOutput").ap()
    gnn_kernel(nc, *args, out)
    r = run_bass_kernel_spmd(nc, [{n + "_dram": a for n, a in arrays.items()}], core_ids=[0])
    return np.ascontiguousarray(r.results[0]["out_dram"].transpose(1, 0, 2))
```

```python
from contextlib import ExitStack

import concourse.bass as bass
from concourse import mybir

F32 = mybir.dt.float32
F16 = mybir.dt.float16
I32 = mybir.dt.int32
ALU = mybir.AluOpType
ACT = mybir.ActivationFunctionType
AX_X = mybir.AxisListType.X

EPS = 1e-5
SLOTS = 4
BANKS = 2
PER_BANK = SLOTS // BANKS
ROW_SLOTS = 3
RING = 3
REGULAR = 4
CHUNKS = REGULAR + 1
COVERED = REGULAR * SLOTS
PARTS = 8
GROUP = 2
QUAD = 4
HOT_RING = 6
BODY = 12
STORE = 4


def gnn_kernel(nc, x, adjT, W1a, W1b, b1, W2, b2, W3T, CONSTS, out):
    N, B, F = x.shape
    H = W1a.shape[1]
    O = W2.shape[1]
    H2 = H - N
    ROW = PER_BANK * H
    PER_PART = B // PARTS
    QUADS = PER_PART // QUAD
    GROUPS = PARTS // GROUP
    LOOPED = (N - COVERED) // SLOTS
    RECIPROCAL = 4096 // (2 * ROW_SLOTS) + 1
    assert N == 128 and 2 * F == N and B == N and F == O and N < H <= 256 and ROW <= 512 and 2 * H + 2 * O <= 512 and 4 * N <= 512
    assert BODY % 2 == 0 and CHUNKS * BODY % RING == 0 and REGULAR * BODY // 2 % HOT_RING == 0 and HOT_RING == REGULAR + 2 and ROW_SLOTS <= SLOTS and PER_BANK * H <= 512 and QUADS + 2 <= RING * BANKS

    with ExitStack() as ctx:
        def sb(name, shape, dt=F32):
            return ctx.enter_context(nc.sbuf_tensor(name, shape, dt))

        def sem(name):
            return ctx.enter_context(nc.semaphore(name))

        x_all = sb("x_all", [N, B, F])
        adj_all = sb("adj_all", [N, B, N])
        mask_all = sb("mask_all", [N, B, N], F16)
        code_kj = mask_all
        code_jk = sb("code_jk", [N, B, N], F16)
        w_parts = sb("w_parts", [N, 2, 3 * H], F16)
        w2a = sb("w2a", [N, O])
        w2b = sb("w2b", [H2, O])
        w3t = sb("w3t", [F, O])
        b2_rows = sb("b2_rows", [N, O])
        consts = sb("consts", [N, 3, N])
        before, ident, count = consts[:, 0, :], consts[:, 1, :], consts[:, 2, :]
        loop_codes = sb("loop_codes", [N, SLOTS])
        to_scale = sb("to_scale", [N, 4])
        to_scale_i = to_scale[:, :].bitcast(I32)
        ones_row = sb("ones_row", [1, N])
        ident_h = sb("ident_h", [N, N], F16)
        count_h = sb("count_h", [N, N], F16)
        ones_h = sb("ones_h", [N, N], F16)
        count_off = sb("count_off", [1, N], F16)
        ones = sb("ones", [N, N])
        half_power = sb("half_power", [N, 1])
        rstd1 = sb("rstd1", [N, B])
        shift1 = sb("shift1", [N, B])
        deg = sb("deg", [N, B])
        all_fit = sb("all_fit", [1, 1])
        any_loops = sb("any_loops", [1, 1], I32)
        loops = sb("loops", [1, 2, B], I32)
        first_row = sb("first_row", [N, B])
        end_row = sb("end_row", [N, B])
        first_code = sb("first_code", [N, B], F16)
        spare = sb("spare", [N, B])
        h1 = sb("h1", [N, 2, F])
        h1_parts = sb("h1_parts", [N, 2, 2, F], F16)
        h1T = sb("h1T", [2 * F, N], F16)
        P = sb("P", [N, 2, H])
        PQ = sb("PQ", [N, 2, 2, 2 * H], F16)
        onehot_space = sb("onehot_space", [N, HOT_RING, SLOTS, N])
        onehot = onehot_space[:, :, :, :].bitcast(F16).rearrange("p c s (g n) -> p c s g n", g=2)
        scratch = onehot_space[:, :, :, :].rearrange("p c s n -> p (c s n)")
        stats1 = scratch[:, 0:6 * B].rearrange("p (b k) -> p b k", k=6)
        rows = scratch[:, 10 * B:11 * B]
        fits = scratch[:, 11 * B:12 * B]
        too_many = scratch[:, 12 * B:13 * B]
        edges_i = scratch[:, 13 * B:14 * B].bitcast(I32)
        rows_i = scratch[:, 14 * B:15 * B].bitcast(I32)
        owned = scratch[:, 15 * B:16 * B]
        upto = scratch[:, 16 * B:17 * B]
        w_pq = scratch[:, 6 * B:6 * B + 3 * H]
        w1b = scratch[:, 19 * B:19 * B + H]
        coder = scratch[:, 21 * B:22 * B].bitcast(F16)[:, 0:N]
        mom = sb("mom", [N, 4, B])
        onehot_row = sb("onehot_row", [N, SLOTS, N], F16)
        from_first = sb("from_first", [N, N], F16)
        owner = sb("owner", [N, 2, N], F16)
        ownerT = sb("ownerT", [N, 2, N])
        code_row = sb("code_row", [N, N], F16)
        start = sb("start", [N, PER_BANK, H])
        acc = sb("acc", [N, 2, BANKS, ROW])
        relu_row = sb("relu_row", [N, ROW_SLOTS, H])
        sums_T = sb("sums_T", [N, 3, N])
        hmT, aggT = sums_T[:, 0:2, :], sums_T[0:F, 2, :]
        bias = sb("bias", [N, F])
        stats2 = sb("stats2", [N, 6])
        mv = sb("mv", [N, 2, 2])
        ve2 = sb("ve2", [N, 1])
        neg2 = sb("neg2", [N, 2])
        rstd2 = sb("rstd2", [N, 2])
        shift2 = sb("shift2", [N, 2])
        h2 = sb("h2", [N, 2, F])

        ring = ctx.enter_context(nc.psum_tensor("ring", [N, RING, BANKS, 512], F32))
        prep = ctx.enter_context(nc.psum_tensor("prep", [N, 512], F32))
        post = ctx.enter_context(nc.psum_tensor("post", [N, 512], F32))
        slots = [ring[:, k, :, :].rearrange("p a (s w) -> p a s w", s=PER_BANK)[:, :, :, 0:H] for k in range(RING)]
        row_slots = [ring[:, k, :, :].rearrange("p a (s w) -> p (a s) w", s=PER_BANK)[:, 0:ROW_SLOTS, 0:H] for k in range(RING)]
        bank = [ring[:, k // BANKS, k % BANKS, :] for k in range(RING * BANKS)]
        tables = bank[-1].rearrange("p (k b) -> p k b", b=B)
        pq_ps, out1_ps, out2_ps = prep[:, 0:2 * H], prep[:, 2 * H:2 * H + O], prep[:, 2 * H + O:2 * H + 2 * O]
        sums_T_ps = post[:, 0:3 * N].rearrange("p (k n) -> p k n", k=3)
        h1T_ps = post[:, 3 * N:4 * N]
        code_row_ps, ownerT_ps = post[:, 0:N], post[:, N:2 * N]

        consts_in = sem("consts_in")
        first_weights_in = sem("first_weights_in")
        weights_in = sem("weights_in")
        x_in = [sem(f"x_in{g}") for g in range(PARTS)]
        adj_in = [sem(f"adj_in{g}") for g in range(PARTS)]
        weights_ready = sem("weights_ready")
        mask_ready = sem("mask_ready")
        codes_summed = sem("codes_summed")
        code_kj_ready = sem("code_kj_ready")
        code_jk_ready = sem("code_jk_ready")
        late_codes_ready = sem("late_codes_ready")
        largest_ready = sem("largest_ready")
        largest_seen = sem("largest_seen")
        rows_counted = sem("rows_counted")
        owned_ready = sem("owned_ready")
        owned_sums = sem("owned_sums")
        any_loops_ready = sem("any_loops_ready")
        tables_ready = sem("tables_ready")
        ring_ready = sem("ring_ready")
        stats1_ready = sem("stats1_ready")
        moments_ready = sem("moments_ready")
        norm1_ready = sem("norm1_ready")
        dve_step = sem("dve_step")
        pool_step = sem("pool_step")
        h1_ready = sem("h1_ready")
        transposed = sem("transposed")
        mixed = sem("mixed")
        h1_part_ready = sem("h1_part_ready")
        h1_split = sem("h1_split")
        h1T_ready = sem("h1T_ready")
        p_ready = sem("p_ready")
        pq_ready = sem("pq_ready")
        p_part_ready = sem("p_part_ready")
        start_ready = sem("start_ready")
        onehot_ready = sem("onehot_ready")
        from_ready = sem("from_ready")
        owner_ready = sem("owner_ready")
        rows_summed = sem("rows_summed")
        rows_ready = sem("rows_ready")
        onehot_row_ready = sem("onehot_row_ready")
        seeded = sem("seeded")
        gathered = sem("gathered")
        summed = sem("summed")
        relu_row_ready = sem("relu_row_ready")
        onehot_loop_ready = sem("onehot_loop_ready")
        loop_codes_ready = sem("loop_codes_ready")
        loop_seeded = sem("loop_seeded")
        loop_gathered = sem("loop_gathered")
        loop_summed = sem("loop_summed")
        half_ready = sem("half_ready")
        hm_ready = sem("hm_ready")
        half_row_ready = sem("half_row_ready")
        hm_row_ready = sem("hm_row_ready")
        sums_T_ready = sem("sums_T_ready")
        bias_ready = sem("bias_ready")
        xb_ready = sem("xb_ready")
        x1_ready = sem("x1_ready")
        stats2_ready = sem("stats2_ready")
        mv_ready = sem("mv_ready")
        ve2_ready = sem("ve2_ready")
        rstd2_ready = sem("rstd2_ready")
        neg2_ready = sem("neg2_ready")
        norm2_ready = sem("norm2_ready")
        h2_ready = sem("h2_ready")
        y_ready = sem("y_ready")
        stored = sem("stored")

        HOT_AT = ((0, 1, 2, 4), (1, 2, 3, 4))
        HEAD, TAIL = 3, 4
        LATE = PARTS - 1

        def lead(step, lo=-HEAD, hi=0):
            for b in range(lo, hi):
                step(b, b % BODY)

        def load_any(eng):
            eng.wait_ge(any_loops_ready, 1)
            return eng.snap(eng.value_load(any_loops[0:1, 0:1], min_val=0, max_val=1))

        def graphs(eng, step, some):
            rounds = (B - HEAD) // BODY
            for looped in (False, True):
                with eng.If(some > 0 if looped else some < 1):
                    for b in range(BODY):
                        step(b, b, looped)
                    with eng.Fori(1, rounds) as t:
                        for u in range(BODY):
                            step(t * BODY + u, u, looped)
                    for b in range(rounds * BODY, B + TAIL):
                        step(b, b % BODY, looped)

        def exists(b):
            return not isinstance(b, int) or 0 <= b < B

        def place(u, i):
            return (CHUNKS * u + i) % RING

        def hot_place(pair, i):
            return (REGULAR * pair + i) % HOT_RING

        def load(eng, which, b):
            return eng.value_load(loops[0:1, which, bass.ds(b, 1)], min_val=0,
                                  max_val=LOOPED * (1 if which else B))

        until = {}
        for eng in (nc.tensor, nc.scalar, nc.vector, nc.gpsimd):
            until[eng.engine] = eng.alloc_register("until")

        def wait_apart(eng, semaphore, value):
            if not isinstance(value, int):
                eng.reg_mov(until[eng.engine], value)
                eng.wait_ge(weights_ready, 1)
                value = until[eng.engine]
            eng.wait_ge(semaphore, value)

        block = ctx.enter_context(nc.Block())

        @block.sync
        def _(sp):
            sp.dma_start(consts[:, :, :], CONSTS).then_inc(consts_in, 16)
            for g in range(PARTS):
                b = slice(g * PER_PART, (g + 1) * PER_PART)
                sp.dma_start(adj_all[:, b, :], adjT[:, b, :]).then_inc(adj_in[g], 16)
                sp.dma_start(x_all[:, b, :], x[:, b, :]).then_inc(x_in[g], 16)
            with sp.Fori(0, B // STORE) as t:
                sp.wait_ge(y_ready, t * STORE + STORE)
                b = bass.ds(t * STORE, STORE)
                sp.dma_start(out[:, b, :], x_all[:, b, :]).then_inc(stored, 16)
            sp.wait_ge(stored, 16 * B // STORE)

        @block.tensor
        def _(pe):
            def codes(g):
                pe.wait_ge(mask_ready, g + 1)
                for q in range(QUADS):
                    quad = g * QUADS + q
                    later = not isinstance(g, int) or g > 0
                    if later:
                        pe.wait_ge(code_kj_ready, quad - QUADS + 1)
                    nc.tensor.matmul(bank[q], coder, mask_all[:, bass.ds(QUAD * quad, QUAD), :], start=True, stop=True)
                    if q >= 2 or later:
                        if isinstance(g, int) and quad - 2 >= LATE * QUADS:
                            pe.wait_ge(late_codes_ready, quad - 2 - LATE * QUADS + 1)
                        else:
                            pe.wait_ge(code_jk_ready, quad - 2 + 1)
                    for i in range(QUAD):
                        mask = mask_all[:, QUAD * quad + i, :]
                        last = nc.tensor.matmul(bank[QUADS + q % 2][:, i * N:(i + 1) * N], mask, coder, start=True, stop=True)
                    last.then_inc(codes_summed, 1)

            codes(0)
            codes(1)
            pe.wait_ge(largest_ready, 1)
            nc.tensor.matmul(post[0:1, 0:N], to_scale[:, 0:1], ident, start=True,
                             stop=True).then_inc(largest_seen, 1)
            pe.wait_ge(largest_ready, 2)
            nc.tensor.matmul(post[:, N:N + 1], ones_row[:, :], to_scale[0:1, 1:2], start=True, stop=True).then_inc(largest_seen, 1)
            with pe.Fori(2, LATE) as g:
                codes(g)
            pe.wait_ge(weights_ready, 2)

            def slot(to, s):
                return slots[to][:, s // PER_BANK, s % PER_BANK, :]

            def gather(dst, parts, hot):
                for s, to in enumerate(dst):
                    for part in range(2):
                        last = nc.tensor.matmul(to, hot(s), parts[:, part, H:2 * H], start=False, stop=(part == 1),
                                                skip_group_check=True)
                return last

            def step(b, u, looped=False):
                main = exists(b)
                parts = PQ[:, u % 2]
                for i in range(CHUNKS):
                    if main:
                        if i == 0:
                            pe.wait_ge(pq_ready, b + 1)
                        if i < REGULAR:
                            if u % 2 == 0:
                                pe.wait_ge(onehot_ready, b * (REGULAR // 2) + i + 1)
                            dst = [slot(place(u, i), s) for s in range(SLOTS)]
                            hot = lambda s: onehot[:, hot_place(u // 2, i), s, u % 2, :]
                            pe.wait_ge(seeded, b * REGULAR + i + 1)
                        else:
                            pe.wait_ge(p_part_ready, b + 1)
                            pe.wait_ge(summed, b * REGULAR + 2)
                            dst = [row_slots[place(u, i)][:, s, :] for s in range(ROW_SLOTS)]
                            for bank_ in range(BANKS):
                                for part in range(2):
                                    n = min(PER_BANK, ROW_SLOTS - PER_BANK * bank_) if part else PER_BANK
                                    nc.tensor.matmul(slots[place(u, i)][:, bank_, 0:n, :], owner[:, u % 2, :],
                                                     parts[:, part, 0:H].unsqueeze(1).broadcast_to([N, n, H]),
                                                     start=(part == 0), stop=False, skip_group_check=True)
                            pe.wait_ge(onehot_row_ready, b + 1)
                            hot = lambda s: onehot_row[:, s, :]
                        gather(dst, parts, hot).then_inc(gathered, 1)
                    if i == 0 and main:
                        pe.wait_ge(owner_ready, b + 1)
                        if exists(b - 2):
                            pe.wait_ge(sums_T_ready, b - 1)
                        else:
                            pe.wait_ge(h1T_ready, b + 2)
                        own = owner[:, u % 2, :]
                        nc.tensor.matmul(code_row_ps, code_jk[:, b, :], own, start=True, stop=False)
                        nc.tensor.matmul(code_row_ps, first_code[:, bass.ds(b, 1)].broadcast_to([N, N]), own, start=False, stop=False)
                        nc.tensor.matmul(code_row_ps, ones_h[0:1, :], count_off[:, :], start=False, stop=True)
                        nc.tensor.matmul(ownerT_ps, own, ident_h[:, :], start=True, stop=True).then_inc(rows_summed, 1)
                    if i == 1:
                        if exists(b - 5):
                            pe.wait_ge(y_ready, b - 4)
                        elif exists(b - 3):
                            pe.wait_ge(x1_ready, b - 2)
                        elif exists(b):
                            pe.wait_ge(pq_ready, b + 1)
                        if exists(b + 1):
                            pe.wait_ge(h1T_ready, b + 2)
                            for part in range(2):
                                nc.tensor.matmul(pq_ps, h1T[:, :], w_parts[:, part, 0:2 * H], start=(part == 0), stop=False,
                                                 skip_group_check=True)
                            last = nc.tensor.matmul(pq_ps[:, 0:H], ones_h[:, :], w_parts[:, 0, 2 * H:3 * H], start=False, stop=True,
                                                    skip_group_check=True)
                        if exists(b - 2):
                            pe.wait_ge(sums_T_ready, b - 1)
                            nc.tensor.matmul(out1_ps, hmT[:, 0, :], w2a[:, :], start=True, stop=False)
                            last = nc.tensor.matmul(out1_ps, hmT[0:H2, 1, :], w2b[:, :], start=False, stop=True)
                        if exists(b - 4):
                            pe.wait_ge(sums_T_ready, b - 1)
                            last = nc.tensor.matmul(out2_ps, aggT[:, :], w3t[:, :], start=True, stop=True)
                        if exists(b + 1) or exists(b - 2) or exists(b - 4):
                            last.then_inc(mixed, 1)
                    if i == 3:
                        if main:
                            pe.wait_ge(rows_ready, b + 1)
                        if exists(b + 2):
                            pe.wait_ge(h1_split, b + 3)
                            last = nc.tensor.matmul(h1T_ps, h1_parts[:, u % 2, :, :], ident_h[:, :], start=True, stop=True)
                        if exists(b - 1):
                            pe.wait_ge(hm_ready, b)
                            pe.wait_ge(hm_row_ready, b)
                            hm, hm_row = acc[:, (u + 1) % 2, 0, :], relu_row[:, :, :].rearrange("p s h -> p (s h)")
                            for k, h in enumerate((slice(0, N), slice(N, 2 * N))):
                                nc.tensor.matmul(sums_T_ps[:, k, :], hm[:, h], ident, start=True, stop=False)
                                last = nc.tensor.matmul(sums_T_ps[:, k, :], hm_row[:, h], ownerT[:, (u + 1) % 2, :], start=False, stop=True)
                        if exists(b - 3):
                            pe.wait_ge(h2_ready, b - 2)
                            last = nc.tensor.matmul(sums_T_ps[:, 2, :], h2[:, :, :], adj_all[:, b - 3, :], start=True, stop=True)
                        if exists(b + 2) or exists(b - 1) or exists(b - 3):
                            last.then_inc(transposed, 1)
                if main and looped:
                    first, n = load(nc.tensor, 0, b), load(nc.tensor, 1, b)
                    with nc.tensor.If(n > 0):
                        with nc.tensor.Fori(0, n) as k:
                            pe.wait_ge(onehot_loop_ready, first + k + 1)
                            pe.wait_ge(loop_seeded, first + k + 1)
                            gather([slot(place(u, CHUNKS), s) for s in range(SLOTS)], parts, lambda s: onehot_row[:, s, :]).then_inc(loop_gathered, 1)

            lead(step, hi=-1)
            codes(LATE)
            lead(step, lo=-1)
            for g in range(LATE + 1, PARTS):
                codes(g)
            pe.wait_ge(rows_counted, 1)
            nc.tensor.matmul(tables[:, 0, :], ones[:, :], rows, start=True, stop=True)
            nc.tensor.matmul(tables[:, 1, :], rows, ones[:, :], start=True, stop=True).then_inc(rows_summed, 1)
            def write_ring(banks):
                for k in banks:
                    last = nc.tensor.matmul(bank[k], ident_h[:, :], code_jk[:, 0:QUAD, :], start=True, stop=True)
                return last

            pe.wait_ge(code_kj_ready, B // QUAD)
            pe.wait_ge(late_codes_ready, (PARTS - LATE) * QUADS)
            write_ring(range(QUADS))
            pe.wait_ge(owned_ready, 1)
            nc.tensor.matmul(tables[:, 2, :], upto, owned, start=True, stop=True)
            nc.tensor.matmul(tables[:, 3, :], too_many, before, start=True, stop=True).then_inc(owned_sums, 1)
            write_ring(range(QUADS, RING * BANKS - 1))
            some = load_any(nc.tensor)
            pe.wait_ge(tables_ready, 1)
            write_ring([RING * BANKS - 1]).then_inc(ring_ready, 1)
            graphs(nc.tensor, step, some)

        @block.scalar
        def _(act):
            with nc.allow_non_contiguous_dma("small weights"):
                for dst, src in ((w_pq[0:F, 0:H], W1a), (w_pq[F:2 * F, 0:H], W1a), (w1b[0:F], W1b), (w1b[F:2 * F], W1b),
                                 (w_pq[:, 2 * H:3 * H], b1.partition_broadcast(N))):
                    act.dma_start(dst, src).then_inc(first_weights_in, 16)
                for dst, src in ((w2a[:, :], W2[0:N, :]), (w2b[:, :], W2[N:H, :]), (w3t[:, :], W3T),
                                 (b2_rows[:, :], b2.partition_broadcast(N))):
                    act.dma_start(dst, src).then_inc(weights_in, 16)

            def codes(g):
                for q in range(QUADS):
                    quad = g * QUADS + q
                    b = bass.ds(QUAD * quad, QUAD)
                    wait_apart(act, codes_summed, quad + 1)
                    nc.scalar.copy(code_kj[:, b, :], bank[q].rearrange("p (b j) -> p b j", b=QUAD)).then_inc(code_kj_ready, 1)
                    if not isinstance(g, int) or g < LATE:
                        nc.scalar.copy(code_jk[:, b, :], bank[QUADS + q % 2].rearrange("p (b k) -> p b k", b=QUAD)).then_inc(code_jk_ready, 1)

            def seed(to, src):
                return nc.scalar.copy(slots[to], src.unsqueeze(1).unsqueeze(1).broadcast_to([N, BANKS, PER_BANK, H]))

            def start_sums(b):
                nc.scalar.activation(start[:, 0, :], pq_ps[:, 0:H], ACT.Relu, scale=spare[:, bass.ds(b, 1)]).then_inc(start_ready, 1)

            def step(b, u, looped=False):
                main = exists(b)
                for i in range(CHUNKS):
                    if main and i < REGULAR:
                        if i == 0:
                            act.wait_ge(p_ready, b + 1)
                        if i in (0, 1) and exists(b - 1):
                            act.wait_ge(summed, b * REGULAR - 1 + i)
                        if i == 2 and exists(b - 1):
                            act.wait_ge(relu_row_ready, b)
                        if i == 3:
                            act.wait_ge(summed, b * REGULAR + 1)
                        seed(place(u, i), P[:, u % 2, :]).then_inc(seeded, 1)
                    if i == 0 and exists(b + 1):
                        act.wait_ge(transposed, b + 2)
                        if main:
                            act.wait_ge(mixed, b + 1)
                        nc.scalar.copy(h1T[:, :], h1T_ps).then_inc(h1T_ready, 1)
                    if i == 0 and (exists(b - 2) or exists(b - 4)):
                        act.wait_ge(transposed, b + 2)
                        if exists(b - 3) or exists(b - 5):
                            act.wait_ge(mixed, b + 1)
                        parts = slice(0 if exists(b - 2) else 2, 3 if exists(b - 4) else 2)
                        nc.scalar.copy(sums_T[:, parts, :], sums_T_ps[:, parts, :]).then_inc(sums_T_ready, 1)
                    if i == 1 and exists(b - 1):
                        act.wait_ge(gathered, b * CHUNKS)
                        if exists(b - 2):
                            act.wait_ge(transposed, b + 2)
                        nc.scalar.activation(relu_row[:, :, :], row_slots[place(u, -1)], ACT.Relu).then_inc(relu_row_ready, 1)
                    if i == 1 and main:
                        act.wait_ge(rows_summed, b + 2)
                        if exists(b - 1):
                            act.wait_ge(onehot_row_ready, b)
                        nc.scalar.copy(code_row[:, :], code_row_ps)
                        if exists(b - 2):
                            act.wait_ge(transposed, b + 2)
                        nc.scalar.copy(ownerT[:, u % 2, :], ownerT_ps).then_inc(rows_ready, 1)
                    if i == 3 and exists(b + 1):
                        act.wait_ge(mixed, b + 2)
                        if exists(b - 1):
                            act.wait_ge(gathered, b * CHUNKS)
                        nc.scalar.copy(PQ[:, (u + 1) % 2, 0, :], pq_ps)
                        nc.scalar.copy(P[:, (u + 1) % 2, :], pq_ps[:, 0:H]).then_inc(p_ready, 1)
                        if main:
                            start_sums(b + 1)
                    if i == 4 and exists(b - 3):
                        k = (u + 1) % 2
                        wait_apart(act, norm2_ready, b - 2)
                        if exists(b - 4):
                            act.wait_ge(transposed, b + 2)
                        nc.scalar.activation(h2[:, 0, :], x_all[:, b - 3, :], ACT.Relu, bias=shift2[:, k:k + 1],
                                             scale=rstd2[:, k:k + 1]).then_inc(h2_ready, 1)
                    if i == 4 and exists(b + 3):
                        if isinstance(b, int) and b == 0:
                            act.wait_ge(norm1_ready, GROUPS)
                        if exists(b + 1):
                            act.wait_ge(transposed, b + 2)
                        nc.scalar.activation(h1[:, (u + 1) % 2, :], x_all[:, b + 3, :], ACT.Relu, bias=shift1[:, bass.ds(b + 3, 1)],
                                             scale=rstd1[:, bass.ds(b + 3, 1)]).then_inc(h1_ready, 1)
                if main and looped:
                    first, n = load(nc.scalar, 0, b), load(nc.scalar, 1, b)
                    with nc.scalar.If(n > 0):
                        act.wait_ge(summed, b * REGULAR + 3)
                        with nc.scalar.Fori(0, n) as k:
                            wait_apart(act, loop_summed, first + k + 1)
                            seed(place(u, CHUNKS), P[:, u % 2, :]).then_inc(loop_seeded, 1)
                        wait_apart(act, loop_summed, first + n + 1)
                        act.reg_mov(until[act.engine], first + n)

            codes(0)
            with nc.scalar.Fori(1, LATE // 2) as g:
                codes(g)
            act.wait_ge(norm1_ready, 1)
            lead(step, hi=-2)
            with nc.scalar.Fori(LATE // 2, LATE) as g:
                codes(g)
            lead(step, lo=-2, hi=-1)
            codes(LATE)
            lead(step, lo=-1)
            for g in range(LATE + 1, PARTS):
                codes(g)
            some = load_any(nc.scalar)
            act.wait_ge(tables_ready, 1)
            act.wait_ge(pq_ready, 1)
            start_sums(0)
            act.wait_ge(ring_ready, 1)
            graphs(nc.scalar, step, some)

        @block.vector
        def _(dve):
            done = [0]

            def chain(ins):
                done[0] += 1
                ins.then_inc(dve_step, 1)
                dve.wait_ge(dve_step, done[0])

            nc.vector.memset(ones[:, :], 1.0)
            nc.vector.memset(ones_row[:, :], 1.0)
            nc.vector.memset(half_power[:, :], -0.5)
            nc.vector.memset(ones_h[:, :], 1.0)
            nc.vector.memset(h2[:, 1, :], 0.0)
            nc.vector.memset(start[:, :, :], 0.0).then_inc(loop_summed, 1)
            dve.wait_ge(consts_in, 16)
            nc.vector.tensor_tensor(upto, before, ident, ALU.add)
            nc.vector.scalar_tensor_tensor(coder, before, 2.0, ident, ALU.mult, ALU.add)
            nc.vector.tensor_scalar(count_h[:, :], count, 1.0, None, ALU.mult)
            nc.vector.tensor_scalar(count_off[:, :], count[0:1, :], -2.0 * ROW_SLOTS, None, ALU.mult)
            nc.vector.tensor_scalar(ident_h[:, :], ident, 1.0, None, ALU.mult).then_inc(weights_ready, 1)
            def mask(g):
                b = slice(g * PER_PART, (g + 1) * PER_PART)
                dve.wait_ge(adj_in[g], 16)
                nc.vector.tensor_scalar(mask_all[:, b, :], adj_all[:, b, :], 0.0, None, ALU.is_gt).then_inc(mask_ready, 1)

            def scale():
                dve.wait_ge(first_weights_in, 16 * 5)
                nc.vector.tensor_scalar(w_pq[:, H:2 * H], w1b, -1.0, None, ALU.mult)
                chain(nc.vector.tensor_tensor(w_pq[:, 0:H], w_pq[:, 0:H], w1b, ALU.add))
                nc.vector.tensor_reduce(to_scale[:, 0:1], w_pq[:, :], AX_X, ALU.max, apply_absolute_value=True).then_inc(largest_ready, 1)
                dve.wait_ge(largest_seen, 1)
                nc.vector.tensor_reduce(to_scale[0:1, 1:2], post[0:1, 0:N], AX_X, ALU.max).then_inc(largest_ready, 1)
                dve.wait_ge(largest_seen, 2)
                chain(nc.vector.tensor_copy(to_scale[:, 2:3], post[:, N:N + 1]))
                exponent = 1 << 23
                chain(nc.vector.tensor_scalar(to_scale_i[:, 3:4], to_scale_i[:, 2:3], 255 * exponent, None, ALU.bitwise_and))
                chain(nc.vector.tensor_scalar(to_scale_i[:, 3:4], to_scale_i[:, 3:4], float((127 - 100) * exponent), None, ALU.max))
                nc.vector.tensor_scalar(to_scale_i[:, 2:3], to_scale_i[:, 3:4], -1.0, float((2 * 127 + 8 - (F.bit_length() - 1)) * exponent), ALU.mult, ALU.add)
                chain(nc.vector.tensor_scalar(to_scale_i[:, 3:4], to_scale_i[:, 3:4], float(-8 * exponent), None, ALU.add))
                chain(nc.vector.tensor_scalar(w_parts[:, 0, :], w_pq[:, :], to_scale[:, 2:3], None, ALU.mult))
                chain(nc.vector.scalar_tensor_tensor(w_parts[:, 1, :], w_pq[:, :], to_scale[:, 2:3], w_parts[:, 0, :], ALU.mult,
                                                     ALU.subtract))
                nc.vector.tensor_copy(w_parts[F:2 * F, 0, 2 * H:3 * H], w_parts[F:2 * F, 1, 2 * H:3 * H]).then_inc(weights_ready, 1)

            def late_codes(g):
                for q in range(QUADS):
                    b = slice((g * QUADS + q) * QUAD, (g * QUADS + q + 1) * QUAD)
                    dve.wait_ge(codes_summed, g * QUADS + q + 1)
                    nc.vector.tensor_copy(code_jk[:, b, :], bank[QUADS + q % 2].rearrange("p (b k) -> p b k", b=QUAD)).then_inc(late_codes_ready, 1)

            def second_part(b, u):
                nc.vector.tensor_tensor(PQ[:, u % 2, 1, H:2 * H], pq_ps[:, H:2 * H], PQ[:, u % 2, 0, H:2 * H],
                                        ALU.subtract).then_inc(pq_ready, 1)

            m_even, m_odd, s_even, s_odd = (stats1[:, :, k] for k in (1, 4, 2, 5))
            for g in range(PARTS):
                mask(g)
                if g > LATE:
                    late_codes(g - 1)
                dve.wait_ge(x_in[g], 16)
                for b in range(g * PER_PART, (g + 1) * PER_PART):
                    stats = nc.vector.bn_stats(stats1[:, b, :], x_all[:, b, :])
                if g % GROUP < GROUP - 1:
                    continue
                stats.then_inc(stats1_ready, 1)
                if g == 1:
                    scale()
                dve.wait_ge(stats1_ready, g // GROUP + 1)
                b = slice((g - GROUP + 1) * PER_PART, (g + 1) * PER_PART)
                nc.vector.tensor_tensor(mom[:, 0, b], m_even[:, b], m_odd[:, b], ALU.add)
                nc.vector.tensor_tensor(mom[:, 1, b], m_even[:, b], m_odd[:, b], ALU.subtract)
                chain(nc.vector.tensor_tensor(mom[:, 2, b], s_even[:, b], s_odd[:, b], ALU.add))
                nc.vector.tensor_scalar(mom[:, 0, b], mom[:, 0, b], -0.5, None, ALU.mult)
                nc.vector.tensor_scalar(mom[:, 2, b], mom[:, 2, b], 1.0 / F**3, EPS / F**2, ALU.mult, ALU.add)
                chain(nc.vector.scalar_tensor_tensor(mom[:, 3, b], mom[:, 1, b], 0.25 / F**2, mom[:, 1, b], ALU.mult, ALU.mult))
                nc.vector.tensor_tensor(mom[:, 3, b], mom[:, 3, b], mom[:, 2, b], ALU.add).then_inc(moments_ready, 1)

            dve.wait_ge(weights_in, 16 * 4)
            nc.vector.tensor_scalar(w2a[:, :], w2a[:, :], to_scale[:, 3:4], None, ALU.mult)
            nc.vector.tensor_scalar(w2b[:, :], w2b[:, :], to_scale[0:H2, 3:4], None, ALU.mult).then_inc(weights_ready, 1)
            late_codes(PARTS - 1)
            dve.wait_ge(code_jk_ready, LATE * QUADS)
            dve.wait_ge(late_codes_ready, (PARTS - LATE) * QUADS)
            chain(nc.vector.tensor_scalar(rows_i, code_jk[:, :, N - 1], float(1 + 2 * (ROW_SLOTS - 1 - COVERED)), float(RECIPROCAL),
                                          ALU.add, ALU.mult))
            chain(nc.vector.tensor_scalar(rows_i, rows_i, 12, None, ALU.arith_shift_right))
            nc.vector.tensor_scalar(rows, rows_i, 0.0, None, ALU.max).then_inc(rows_counted, 1)
            chain(nc.vector.tensor_scalar(edges_i, code_jk[:, :, N - 1], 1.0, None, ALU.add))
            chain(nc.vector.tensor_scalar(edges_i, edges_i, 1, None, ALU.arith_shift_right))
            chain(nc.vector.tensor_copy(deg[:, :], edges_i))
            dve.wait_ge(p_ready, 1)
            second_part(0, 0)
            dve.wait_ge(rows_summed, 1)
            dve.wait_ge(rows_counted, 1)
            chain(nc.vector.tensor_scalar(fits, tables[:, 0, :], float(N), None, ALU.is_le))
            nc.vector.tensor_scalar(too_many, tables[:, 1, :], float(N), None, ALU.is_gt)
            nc.vector.tensor_tensor(owned, rows, fits, ALU.mult).then_inc(owned_ready, 1)
            dve.wait_ge(owned_ready, 1)
            chain(nc.vector.tensor_reduce(all_fit[:, :], fits[0:1, :], AX_X, ALU.min))
            nc.vector.tensor_scalar(any_loops[:, :], all_fit[:, :], -1.0, 1.0, ALU.mult, ALU.add).then_inc(any_loops_ready, 1)
            chain(nc.vector.scalar_tensor_tensor(spare[:, :], owned, -float(ROW_SLOTS), deg[:, :], ALU.mult, ALU.add))
            chain(nc.vector.scalar_tensor_tensor(spare[:, :], fits, float(SLOTS * LOOPED), spare[:, :], ALU.mult, ALU.add))
            chain(nc.vector.tensor_scalar(spare[:, :], spare[:, :], -float(COVERED + SLOTS * LOOPED), -1.0 / BANKS, ALU.add, ALU.mult))
            nc.vector.tensor_scalar(loops[0:1, 1, :], fits[0:1, :], -float(LOOPED), float(LOOPED), ALU.mult, ALU.add)
            dve.wait_ge(owned_sums, 1)
            nc.vector.tensor_scalar(loops[0:1, 0, :], tables[0:1, 3, :], float(LOOPED), None, ALU.mult)
            nc.vector.tensor_copy(end_row[:, :], tables[:, 2, :])
            chain(nc.vector.tensor_tensor(first_row[:, :], tables[:, 2, :], owned, ALU.subtract))
            nc.vector.tensor_scalar(first_code[:, :], first_row[:, :], 2.0 * ROW_SLOTS, None, ALU.mult).then_inc(tables_ready, 1)
            dve.wait_ge(tables_ready, 1)

            def hot(b, u, i, s):
                return nc.vector.tensor_scalar(onehot[:, hot_place(u // 2, i), s, :, :], code_kj[:, bass.ds(b, 2), :],
                                               2.0 * (SLOTS * i + s) + 1.0, None, ALU.is_equal)

            def prepare(b, u, i):
                if i in HOT_AT[u % 2] and exists(b - u % 2 + 2):
                    k = u % 2 * REGULAR + HOT_AT[u % 2].index(i)
                    for s in range(2):
                        last = hot(b - u % 2 + 2, u - u % 2 + 2, k // 2, k % 2 * 2 + s)
                        if k % 2 * 2 + s == SLOTS - 1:
                            last.then_inc(onehot_ready, 1)

            def consume(u, to, first):
                sums = acc[:, u % 2].rearrange("p a (s h) -> p a s h", h=H)
                so_far = start[:, :, :].unsqueeze(1).broadcast_to([N, BANKS, PER_BANK, H]) if first else sums
                return nc.vector.scalar_tensor_tensor(sums, slots[to], 0.0, so_far, ALU.max, ALU.subtract if first else ALU.add)

            def step(b, u, looped=False):
                main = exists(b)
                at = bass.ds(b + 1, 1)
                for i in range(CHUNKS):
                    if i < REGULAR:
                        prepare(b, u, i)
                    if i == 3 and main and exists(b + 1):
                        dve.wait_ge(start_ready, b + 2)
                        second_part(b + 1, u + 1)
                    if main and i < REGULAR:
                        if i == 0:
                            dve.wait_ge(start_ready, b + 1)
                            if exists(b - 2):
                                dve.wait_ge(transposed, b + 2)
                        else:
                            dve.wait_ge(summed, b * REGULAR + i)
                        dve.wait_ge(gathered, b * CHUNKS + i + 1)
                        consume(u, place(u, i), i == 0).then_inc(summed, 1)
                    if i == 0 and exists(b - 3):
                        wait_apart(dve, stats2_ready, b - 2)
                        nc.vector.bn_aggr(mv[:, (u + 1) % 2, :], stats2[:, :]).then_inc(mv_ready, 1)
                    if i == 0 and exists(b + 1):
                        if main:
                            dve.wait_ge(owner_ready, b + 1)
                        nc.vector.tensor_scalar(from_first[:, :], count_h[:, :], first_row[:, at], None, ALU.is_ge).then_inc(from_ready, 1)
                    if i == 1 and exists(b + 1):
                        dve.wait_ge(from_ready, b + 2)
                        nc.vector.scalar_tensor_tensor(owner[:, (u + 1) % 2, :], count_h[:, :], end_row[:, at], from_first[:, :], ALU.is_lt,
                                                       ALU.mult).then_inc(owner_ready, 1)
                    if i == 2 and main:
                        dve.wait_ge(rows_ready, b + 1)
                        for s in range(ROW_SLOTS):
                            last = nc.vector.tensor_scalar(onehot_row[:, s, :], code_row[:, :], 2.0 * (COVERED + s) + 1.0, None,
                                                           ALU.is_equal)
                        last.then_inc(onehot_row_ready, 1)
                    if i == 3 and exists(b - 2):
                        dve.wait_ge(xb_ready, b - 1)
                        dve.wait_ge(mixed, b + 2)
                        if exists(b + 1):
                            dve.wait_ge(start_ready, b + 2)
                        nc.vector.tensor_tensor(x_all[:, b - 2, :], x_all[:, b - 2, :], out1_ps, ALU.add).then_inc(x1_ready, 1)
                    if i == 4 and exists(b - 4):
                        dve.wait_ge(mixed, b + 2)
                        nc.vector.tensor_tensor(x_all[:, b - 4, :], x_all[:, b - 4, :], out2_ps, ALU.add).then_inc(y_ready, 1)
                    if i == REGULAR:
                        prepare(b, u, i)
                    if i == 4 and exists(b - 2):
                        wait_apart(dve, x1_ready, b - 1)
                        nc.vector.bn_stats(stats2[:, :], x_all[:, b - 2, :]).then_inc(stats2_ready, 1)
                if main and looped:
                    first, n = load(nc.vector, 0, b), load(nc.vector, 1, b)
                    with nc.vector.If(n > 0):
                        with nc.vector.Fori(0, n) as k:
                            edges = bass.ds(k * SLOTS + COVERED, SLOTS)
                            wait_apart(dve, summed, b * REGULAR + REGULAR)
                            dve.wait_ge(gathered, b * CHUNKS + CHUNKS)
                            nc.vector.tensor_scalar(loop_codes[:, :], count_h[:, edges], 2.0, 1.0, ALU.mult,
                                                    ALU.add).then_inc(loop_codes_ready, 1)
                            wait_apart(dve, loop_codes_ready, first + k + 1)
                            for s in range(SLOTS):
                                last = nc.vector.tensor_scalar(onehot_row[:, s, :], code_kj[:, b, :],
                                                               loop_codes[:, s:s + 1], None, ALU.is_equal)
                            last.then_inc(onehot_loop_ready, 1)
                            dve.wait_ge(loop_summed, first + k + 1)
                            dve.wait_ge(loop_gathered, first + k + 1)
                            consume(u, place(u, CHUNKS), False).then_inc(loop_summed, 1)

            lead(step)
            graphs(nc.vector, step, load_any(nc.vector))

        @block.gpsimd
        def _(pool):
            def step(b, u, looped=False):
                if exists(b - 1):
                    if looped:
                        pool.wait_ge(loop_summed, load(nc.gpsimd, 0, b - 1) + load(nc.gpsimd, 1, b - 1) + 1)
                    pool.wait_ge(summed, b * REGULAR)
                    half = acc[:, (u + 1) % 2, 0, :]
                    nc.gpsimd.tensor_tensor(half, half, acc[:, (u + 1) % 2, 1, :], ALU.add).then_inc(half_ready, 1)
                    pool.wait_ge(half_ready, b)
                    nc.gpsimd.tensor_tensor(half[:, 0:H], half[:, 0:H], half[:, H:2 * H], ALU.add).then_inc(hm_ready, 1)
                if exists(b - 1):
                    pool.wait_ge(relu_row_ready, b)
                    sums = relu_row[:, 0, :]
                    for s in range(1, ROW_SLOTS):
                        last = nc.gpsimd.tensor_tensor(sums, sums, relu_row[:, s, :], ALU.add)
                        if s < ROW_SLOTS - 1:
                            last.then_inc(half_row_ready, 1)
                            pool.wait_ge(half_row_ready, (b - 1) * (ROW_SLOTS - 2) + s)
                    last.then_inc(hm_row_ready, 1)
                if exists(b - 3):
                    k = (u + 1) % 2
                    wait_apart(pool, mv_ready, b - 2)
                    nc.gpsimd.tensor_scalar(ve2[:, :], mv[:, k, 1:2], EPS, None, ALU.add).then_inc(ve2_ready, 1)
                    nc.gpsimd.tensor_scalar(neg2[:, k:k + 1], mv[:, k, 0:1], -1.0, None, ALU.mult).then_inc(neg2_ready, 1)
                    pool.wait_ge(ve2_ready, b - 2)
                    if exists(b - 4):
                        pool.wait_ge(norm2_ready, b - 3)
                    if exists(b - 5):
                        pool.wait_ge(h2_ready, b - 4)
                    nc.gpsimd.tensor_tensor(rstd2[:, k:k + 1], ve2[:, :], half_power[:, :], ALU.pow).then_inc(rstd2_ready, 1)
                    pool.wait_ge(neg2_ready, b - 2)
                    pool.wait_ge(rstd2_ready, b - 2)
                    nc.gpsimd.tensor_tensor(shift2[:, k:k + 1], neg2[:, k:k + 1], rstd2[:, k:k + 1], ALU.mult).then_inc(norm2_ready, 1)
                if exists(b + 1):
                    pool.wait_ge(p_ready, b + 2)
                    nc.gpsimd.tensor_tensor(PQ[:, (u + 1) % 2, 1, 0:H], P[:, (u + 1) % 2, :], PQ[:, (u + 1) % 2, 0, 0:H],
                                            ALU.subtract).then_inc(p_part_ready, 1)
                if exists(b - 1):
                    wait_apart(pool, h1_ready, b)
                    if exists(b - 2):
                        pool.wait_ge(xb_ready, b - 1)
                    nc.gpsimd.tensor_tensor(bias[:, :], b2_rows[:, :], deg[:, bass.ds(b - 1, 1)].broadcast_to([N, F]),
                                            ALU.mult).then_inc(bias_ready, 1)
                    wait_apart(pool, bias_ready, b)
                    nc.gpsimd.tensor_tensor(x_all[:, b - 1, :], x_all[:, b - 1, :], bias[:, :], ALU.add).then_inc(xb_ready, 1)
                if exists(b + 3):
                    if exists(b + 1):
                        pool.wait_ge(transposed, b + 2)
                    wait_apart(pool, h1_ready, b + 4)
                    nc.gpsimd.tensor_scalar(h1_parts[:, (u + 1) % 2, 0, :], h1[:, (u + 1) % 2, :], 1.0, None, ALU.mult).then_inc(h1_part_ready, 1)
                    pool.wait_ge(h1_part_ready, b + 4)
                    nc.gpsimd.tensor_tensor(h1_parts[:, (u + 1) % 2, 1, :], h1[:, (u + 1) % 2, :], h1_parts[:, (u + 1) % 2, 0, :],
                                            ALU.subtract).then_inc(h1_split, 1)

            for g in range(GROUPS):
                b = slice(g * GROUP * PER_PART, (g + 1) * GROUP * PER_PART)
                pool.wait_ge(moments_ready, g + 1)
                nc.gpsimd.tensor_tensor(rstd1[:, b], mom[:, 3, b], half_power[:, :].broadcast_to([N, GROUP * PER_PART]),
                                        ALU.pow).then_inc(pool_step, 1)
                pool.wait_ge(pool_step, g + 1)
                nc.gpsimd.tensor_tensor(shift1[:, b], mom[:, 0, b], rstd1[:, b], ALU.mult).then_inc(norm1_ready, 1)
                if g > 0 and g < GROUPS - 1:
                    lead(step, lo=g - 1 - HEAD, hi=g - HEAD)
                if g == GROUPS - 2:
                    lead(step, lo=g - HEAD)
            some = load_any(nc.gpsimd)
            pool.wait_ge(tables_ready, 1)
            graphs(nc.gpsimd, step, some)


def kernel(x, adj, L0_gnn_W1, L0_gnn_b1, L0_gnn_W2, L0_gnn_b2, L1_gnn_W):
    import numpy as np
    import concourse.bacc as bacc
    from concourse.bass_utils import run_bass_kernel_spmd

    F = x.shape[2]
    N = x.shape[1]
    k = np.arange(N)
    arrays = {
        "x_nbf": np.ascontiguousarray(np.asarray(x).transpose(1, 0, 2)),
        "adj_kbj": np.ascontiguousarray(np.asarray(adj).transpose(2, 0, 1)),
        "w1a": np.ascontiguousarray(np.asarray(L0_gnn_W1)[:F]),
        "w1b": np.ascontiguousarray(np.asarray(L0_gnn_W1)[F:]),
        "b1": np.ascontiguousarray(L0_gnn_b1),
        "w2": np.ascontiguousarray(L0_gnn_W2),
        "b2": np.ascontiguousarray(L0_gnn_b2),
        "w3t": np.ascontiguousarray(np.asarray(L1_gnn_W).T),
        "consts": np.stack([k[:, None] < k, k[:, None] == k, np.broadcast_to(k, (N, N))], 1).astype(np.float32),
    }
    nc = bacc.Bacc("TRN2", target_bir_lowering=False, num_devices=1)
    args = [nc.dram_tensor(n + "_dram", a.shape, mybir.dt.from_np(a.dtype), kind="ExternalInput").ap()
            for n, a in arrays.items()]
    out = nc.dram_tensor("out_dram", arrays["x_nbf"].shape, F32, kind="ExternalOutput").ap()
    gnn_kernel(nc, *args, out)
    r = run_bass_kernel_spmd(nc, [{n + "_dram": a for n, a in arrays.items()}], core_ids=[0])
    return np.ascontiguousarray(r.results[0]["out_dram"].transpose(1, 0, 2))
```
